# Optimizing a Trainium2 kernel written in Bass

```python
import numpy as np
import jax
import jax.numpy as jnp

def _softmax(x, axis=-1):
    return jax.nn.softmax(x, axis=axis)

def _gelu(x):
    return jax.nn.gelu(x, approximate=True)

def _silu(x):
    return jax.nn.silu(x)

def _sigmoid(x):
    return jax.nn.sigmoid(x)

def _layernorm(x, axis=-1, eps=1e-05):
    m = jnp.mean(x, axis=axis, keepdims=True)
    v = jnp.var(x, axis=axis, keepdims=True)
    return (x - m) / jnp.sqrt(v + eps)

def _scatter_add(tgt, idx, src, axis=0):
    return tgt.at[idx].add(src)

def _segment_sum(src, seg, n):
    return jax.ops.segment_sum(src, seg, n)
kernel_name = 'mk_seq_postln_d1_jaxref_r4_fc0ddc'

def setup_inputs(seed: int=0):
    np.random.seed(seed)
    _w = jnp.asarray

    def _L0_attn_setup():
        import jax, jax.numpy as jnp
        import numpy as np
        D_MODEL, D_STATE, D_CONV, D_INNER = (256, 16, 4, 512)
        BATCH, SEQ = (2, 512)
        key = jax.random.key(seed)
        ks = jax.random.split(key, 12)
        s = 0.02
        inp = {'x': jax.random.normal(ks[0], (BATCH, SEQ, D_MODEL), jnp.float32), 'W_in': jax.random.normal(ks[1], (D_MODEL, 2 * D_INNER), jnp.float32) * s, 'b_in': jnp.zeros((2 * D_INNER,), jnp.float32), 'conv_w': jax.random.normal(ks[2], (D_INNER, 1, D_CONV), jnp.float32) * s, 'conv_b': jnp.zeros((D_INNER,), jnp.float32), 'W_x': jax.random.normal(ks[3], (D_INNER, 2 * D_STATE), jnp.float32) * s, 'b_x': jnp.zeros((2 * D_STATE,), jnp.float32), 'W_dt': jax.random.normal(ks[4], (D_INNER, D_INNER), jnp.float32) * s, 'b_dt': jnp.zeros((D_INNER,), jnp.float32), 'A_log': jnp.log(jnp.tile(jnp.arange(1, D_STATE + 1, dtype=jnp.float32), (D_INNER, 1))), 'D': jnp.ones((D_INNER,), jnp.float32), 'W_out': jax.random.normal(ks[5], (D_INNER, D_MODEL), jnp.float32) * s, 'b_out': jnp.zeros((D_MODEL,), jnp.float32)}
        return inp
    _L0_attn_in = _L0_attn_setup()

    def _L0_ffn_setup():
        import jax, jax.numpy as jnp
        import numpy as np
        D_IN, D_HID = (256, 1024)

        def _ternary(key, shape):
            return jax.random.randint(key, shape, -1, 2).astype(jnp.float32)

        def _tlin(x, w, s):
            return jnp.einsum('bsi,oi->bso', x, w) * s
        key = jax.random.key(seed)
        ks = jax.random.split(key, 12)
        inv = lambda fan: 1.0 / np.sqrt(fan).astype(np.float32)
        return {'x': jax.random.normal(ks[0], (4, 512, D_IN), dtype=jnp.float32), 'w1_w': _ternary(ks[1], (D_HID, D_IN)), 'w1_s': jax.random.uniform(ks[2], (D_HID,), dtype=jnp.float32) * inv(D_IN), 'w2_w': _ternary(ks[3], (D_HID, D_IN)), 'w2_s': jax.random.uniform(ks[4], (D_HID,), dtype=jnp.float32) * inv(D_IN), 'h1_w': _ternary(ks[5], (D_HID, D_HID)), 'h1_s': jax.random.uniform(ks[6], (D_HID,), dtype=jnp.float32) * inv(D_HID), 'h2_w': _ternary(ks[7], (D_HID, D_HID)), 'h2_s': jax.random.uniform(ks[8], (D_HID,), dtype=jnp.float32) * inv(D_HID), 'w3_w': _ternary(ks[9], (D_IN, D_HID)), 'w3_s': jax.random.uniform(ks[10], (D_IN,), dtype=jnp.float32) * inv(D_HID)}
    _L0_ffn_in = _L0_ffn_setup()
    _d = {'L0_attn_x': _L0_attn_in['x'], 'L0_attn_W_in': _L0_attn_in['W_in'], 'L0_attn_b_in': _L0_attn_in['b_in'], 'L0_attn_conv_w': _L0_attn_in['conv_w'], 'L0_attn_conv_b': _L0_attn_in['conv_b'], 'L0_attn_W_x': _L0_attn_in['W_x'], 'L0_attn_b_x': _L0_attn_in['b_x'], 'L0_attn_W_dt': _L0_attn_in['W_dt'], 'L0_attn_b_dt': _L0_attn_in['b_dt'], 'L0_attn_A_log': _L0_attn_in['A_log'], 'L0_attn_D': _L0_attn_in['D'], 'L0_attn_W_out': _L0_attn_in['W_out'], 'L0_attn_b_out': _L0_attn_in['b_out'], 'L0_ffn_w1_w': _L0_ffn_in['w1_w'], 'L0_ffn_w1_s': _L0_ffn_in['w1_s'], 'L0_ffn_w2_w': _L0_ffn_in['w2_w'], 'L0_ffn_w2_s': _L0_ffn_in['w2_s'], 'L0_ffn_h1_w': _L0_ffn_in['h1_w'], 'L0_ffn_h1_s': _L0_ffn_in['h1_s'], 'L0_ffn_h2_w': _L0_ffn_in['h2_w'], 'L0_ffn_h2_s': _L0_ffn_in['h2_s'], 'L0_ffn_w3_w': _L0_ffn_in['w3_w'], 'L0_ffn_w3_s': _L0_ffn_in['w3_s']}
    _x0 = _d['L0_attn_x']
    _d['L0_attn_x'] = jax.random.normal(jax.random.fold_in(jax.random.key(seed), 1), (2, 4096, 256), dtype=_x0.dtype)
    del _x0
    return _d

def reference(L0_attn_x, L0_attn_W_in, L0_attn_b_in, L0_attn_conv_w, L0_attn_conv_b, L0_attn_W_x, L0_attn_b_x, L0_attn_W_dt, L0_attn_b_dt, L0_attn_A_log, L0_attn_D, L0_attn_W_out, L0_attn_b_out, L0_ffn_w1_w, L0_ffn_w1_s, L0_ffn_w2_w, L0_ffn_w2_s, L0_ffn_h1_w, L0_ffn_h1_s, L0_ffn_h2_w, L0_ffn_h2_s, L0_ffn_w3_w, L0_ffn_w3_s):

    def _L0_attn_ref(x, W_in, b_in, conv_w, conv_b, W_x, b_x, W_dt, b_dt, A_log, D, W_out, b_out):
        import jax, jax.numpy as jnp
        import numpy as np
        D_MODEL, D_STATE, D_CONV, D_INNER = (256, 16, 4, 512)
        BATCH, SEQ = (2, 512)
        d_inner, d_state = A_log.shape
        d_conv = conv_w.shape[-1]
        bsz, seq_len, _ = x.shape
        xz = x @ W_in + b_in
        xh, z = jnp.split(xz, 2, axis=-1)
        xc = jnp.transpose(xh, (0, 2, 1))
        xc = jax.lax.conv_general_dilated(xc, conv_w, window_strides=(1,), padding=[(d_conv - 1, 0)], dimension_numbers=('NCH', 'OIH', 'NCH'), feature_group_count=d_inner)
        xc = xc + conv_b[None, :, None]
        xh = jax.nn.silu(jnp.transpose(xc, (0, 2, 1)))
        A = -jnp.exp(A_log)
        x_dbl = xh @ W_x + b_x
        Bmat = x_dbl[..., d_state:]
        delta = jax.nn.softplus(xh @ W_dt + b_dt)

        def step(h, inp):
            d_t, b_t, u_t = inp
            dA = jnp.exp(d_t[:, :, None] * A)
            dBu = d_t[:, :, None] * b_t[:, None, :] * u_t[:, :, None]
            h = dA * h + dBu
            return (h, h.sum(-1))
        h0 = jnp.zeros((bsz, d_inner, d_state), x.dtype)
        _, ys = jax.lax.scan(step, h0, (jnp.swapaxes(delta, 0, 1), jnp.swapaxes(Bmat, 0, 1), jnp.swapaxes(xh, 0, 1)))
        y = jnp.swapaxes(ys, 0, 1) + xh * D
        y = y * jax.nn.silu(z)
        return y @ W_out + b_out

    def _L0_ffn_ref(x, w1_w, w1_s, w2_w, w2_s, h1_w, h1_s, h2_w, h2_s, w3_w, w3_s):
        import jax, jax.numpy as jnp
        import numpy as np
        D_IN, D_HID = (256, 1024)

        def _ternary(key, shape):
            return jax.random.randint(key, shape, -1, 2).astype(jnp.float32)

        def _tlin(x, w, s):
            return jnp.einsum('bsi,oi->bso', x, w) * s
        h = jax.nn.silu(_tlin(x, w1_w, w1_s)) * _tlin(x, w2_w, w2_s)
        h = jax.nn.gelu(_tlin(h, h1_w, h1_s), approximate=False)
        h = jax.nn.gelu(_tlin(h, h2_w, h2_s), approximate=False)
        return _tlin(h, w3_w, w3_s)
    x = L0_attn_x
    x = _layernorm(x + _L0_attn_ref(x, L0_attn_W_in, L0_attn_b_in, L0_attn_conv_w, L0_attn_conv_b, L0_attn_W_x, L0_attn_b_x, L0_attn_W_dt, L0_attn_b_dt, L0_attn_A_log, L0_attn_D, L0_attn_W_out, L0_attn_b_out), axis=-1)
    x = _layernorm(x + _L0_ffn_ref(x, L0_ffn_w1_w, L0_ffn_w1_s, L0_ffn_w2_w, L0_ffn_w2_s, L0_ffn_h1_w, L0_ffn_h1_s, L0_ffn_h2_w, L0_ffn_h2_s, L0_ffn_w3_w, L0_ffn_w3_s), axis=-1)
    return x

_drawn_inputs = setup_inputs


def setup_inputs(seed=0):
    import zlib

    import numpy as np

    out = dict(_drawn_inputs(seed))
    spreads = {'L0_attn_b_in': (0.0, 0.8),
     'L0_attn_conv_b': (0.0, 0.8),
     'L0_attn_b_x': (0.0, 0.8),
     'L0_attn_b_dt': (0.0, 0.8),
     'L0_attn_D': (1.0, 0.6),
     'L0_attn_b_out': (0.0, 0.8)}
    factors = {'L0_attn_W_in': 8.0,
     'L0_attn_conv_w': 8.0,
     'L0_attn_W_x': 8.0,
     'L0_attn_W_dt': 8.0,
     'L0_attn_A_log': 8.0,
     'L0_attn_W_out': 8.0,
     'L0_ffn_w1_w': 8.0,
     'L0_ffn_w1_s': 8.0,
     'L0_ffn_w2_w': 8.0,
     'L0_ffn_w2_s': 8.0,
     'L0_ffn_h1_w': 8.0,
     'L0_ffn_h1_s': 8.0,
     'L0_ffn_h2_w': 8.0,
     'L0_ffn_h2_s': 8.0,
     'L0_ffn_w3_w': 8.0,
     'L0_ffn_w3_s': 8.0}
    for name, (base, spread) in spreads.items():
        noise = np.random.default_rng([zlib.crc32(name.encode()), seed]).standard_normal(out[name].shape)
        drawn = base * np.exp(spread * noise) if base else spread * noise
        out[name] = jnp.asarray(drawn.astype(out[name].dtype))
    for name, factor in factors.items():
        out[name] = (out[name] * factor).astype(out[name].dtype)
    return out
```

```python
from contextlib import ExitStack

import concourse.bass as bass
from concourse import mybir

F32 = mybir.dt.float32
ALU = mybir.AluOpType
ACT = mybir.ActivationFunctionType

P = 128
T = 512
TB = T // P
LN_EPS = 1e-5


def mamba_block(nc, w, x, x1, b_scratch):
    NBATCH, SEQ, DM = x.shape
    DI, NS = w["A_log"].shape
    NTAP = w["conv_w"].shape[2]
    G = DI // P
    KM = DM // P
    Q = 4
    NQ = NS // Q
    STEPS = NQ * G
    S = SEQ // T
    NPROJ = 2 * G
    NFRONT = KM + NPROJ + 1 + G
    FB = 3
    PROJ_STEPS = (1, 2, 6, 7)
    assert NBATCH == 2 and NFRONT % FB == 0 and STEPS == 16 and NPROJ == 2 * len(PROJ_STEPS)

    ctx = ExitStack()
    with ctx:
        def sb(name, shape, dt=F32):
            return ctx.enter_context(nc.sbuf_tensor(name, shape, dt))

        def sem(name):
            return ctx.enter_context(nc.semaphore(name))

        w_in = sb("w_in", [P, KM, 2 * DI])
        w_dt = sb("w_dt", [P, G, DI])
        w_b = sb("w_b", [P, G, NS])
        w_out = sb("w_out", [P, G, DM])
        b_in = sb("b_in", [P, NPROJ])
        conv_w = sb("conv_w", [P, G, NTAP])
        conv_b = sb("conv_b", [P, G])
        b_dt = sb("b_dt", [P, G])
        d_skip = sb("d_skip", [P, G])
        b_b = sb("b_b", [NS, 1])
        b_out = sb("b_out", [P, DM])
        a_log = sb("a_log", [P, G, NS])
        a_neg = sb("a_neg", [P, G, NS])
        ident = sb("ident", [P, P])
        x_tok = sb("x_tok", [P, 2, TB, DM])
        xT = sb("xT", [P, KM, T])
        xh_pad = sb("xh_pad", [P, G, NTAP - 1 + T])
        carry = sb("carry", [P, 2, G, NTAP - 1])
        u = sb("u", [P, 2, G, T])
        zs = sb("zs", [P, 2, G, T])
        dt_raw = sb("dt_raw", [P, 2, T])
        dt_exp = sb("dt_exp", [P, 2, T])
        dt_ln = sb("dt_ln", [P, 2, T])
        dt_tmp = sb("dt_tmp", [P, T])
        delta = sb("delta", [P, 2, G, T])
        du = sb("du", [P, 2, G, T])
        b_rows = sb("b_rows", [NS, T])
        b_all = sb("b_all", [P, NS, T])
        decay = sb("decay", [P, 2, Q, T])
        drive = sb("drive", [P, 2, Q, T])
        h = sb("h", [P, 2, Q, T])
        state = sb("state", [P, 2, G, NS])
        r = sb("r", [P, TB, DM])
        stats = sb("stats", [P, TB, 6])
        mv = sb("mv", [P, TB, 2])
        rs = sb("rs", [P, 4, TB])

        ysum = [ctx.enter_context(nc.psum_tensor(f"ysum{g}", [P, T], F32)) for g in range(G)]
        front = [ctx.enter_context(nc.psum_tensor(f"front{i}", [P, T], F32)) for i in range(FB)]
        attn = ctx.enter_context(nc.psum_tensor("attn", [P, 2, DM], F32))

        weights_in = sem("weights_in")
        ident_zero = sem("ident_zero")
        ident_ready = sem("ident_ready")
        a_ready = sem("a_ready")
        a_exp = sem("a_exp")
        x_loaded = [sem(f"x_loaded{b}") for b in range(2)]
        front_full = sem("front_full")
        front_evac = sem("front_evac")
        conv_done = sem("conv_done")
        carried = sem("carried")
        gates = sem("gates")
        act_chain = sem("act_chain")
        dve_chain = sem("dve_chain")
        delta_done = sem("delta_done")
        du_done = sem("du_done")
        b_stored = sem("b_stored")
        b_loaded = [sem(f"b_loaded{q}") for q in range(NQ)]
        decay_done = sem("decay_done")
        drive_done = sem("drive_done")
        scanned = sem("scanned")
        saved = sem("saved")
        h_summed = sem("h_summed")
        y_done = sem("y_done")
        y_evac = sem("y_evac")
        attn_full = sem("attn_full")
        x_used = sem("x_used")
        residual = sem("residual")
        rs_ln = sem("rs_ln")
        var_ready = sem("var_ready")
        x1_ready = sem("x1_ready")
        x1_stored = sem("x1_stored")
        sp_passed = sem("sp_passed")
        dve_passed = sem("dve_passed")

        block = ctx.enter_context(nc.Block())

        weight_loads = [
            (w_in[:], w["W_in"].rearrange("(k p) n -> p k n", p=P)),
            (w_dt[:], w["W_dt"].rearrange("(k p) n -> p k n", p=P)),
            (w_b[:], w["W_x"].rearrange("(k p) n -> p k n", p=P)[:, :, NS:2 * NS]),
            (w_out[:], w["W_out"].rearrange("(k p) n -> p k n", p=P)),
            (b_in[:], w["b_in"].rearrange("(k p) -> p k", p=P)),
            (conv_w[:], w["conv_w"].rearrange("(k p) o t -> p k (o t)", p=P)),
            (conv_b[:], w["conv_b"].rearrange("(k p) -> p k", p=P)),
            (b_dt[:], w["b_dt"].rearrange("(k p) -> p k", p=P)),
            (d_skip[:], w["D"].rearrange("(k p) -> p k", p=P)),
            (b_b[:], w["b_x"].rearrange("(n o) -> n o", o=1)[NS:2 * NS, :]),
            (b_out[:], w["b_out"].rearrange("(o n) -> o n", o=1).broadcast_to([P, DM])),
            (a_log[:], w["A_log"].rearrange("(k p) n -> p k n", p=P)),
        ]
        WEIGHTS = 16 * len(weight_loads)

        def for_tiles(eng, body):
            for b in range(2):
                body(0, b)
            with eng.Fori(1, S - 1) as s:
                for b in range(2):
                    body(s, b)
            for b in range(2):
                body(S - 1, b)

        def is_first(s, b):
            return isinstance(s, int) and s == 0 and b == 0

        def is_last(s, b):
            return isinstance(s, int) and s == S - 1 and b == 1

        def wait(eng, semaphore, value):
            if not (isinstance(value, int) and value <= 0):
                eng.wait_ge(semaphore, value)

        @block.sync
        def _(sp):
            for dst, src in weight_loads:
                sp.dma_start(dst, src, allow_slow_non_contiguous=True).then_inc(weights_in, 16)

            def load_x(s, b):
                sp.dma_start(x_tok[:, b], x[b, bass.ds(s * T, T), :].rearrange("(c p) d -> p c d", p=P)
                             ).then_inc(x_loaded[b], 16)

            def move_b(n, between=lambda: None):
                for q in range(NQ):
                    wait(sp, b_loaded[q], 16 * n)
                wait(sp, front_evac, NFRONT * n + KM + NPROJ + 1)
                sp.dma_start(b_scratch, b_rows[:]).then_inc(b_stored, 16)
                wait(sp, b_stored, 16 * n + 16)
                sp.sem_inc(sp_passed, 1)
                for q in range(NQ):
                    if q == NQ - 1:
                        between()
                    wait(sp, drive_done, STEPS * (n - 1) + (q + 1) * G)
                    sp.dma_start(b_all[:, q * Q:(q + 1) * Q, :],
                                 b_scratch[q * Q:(q + 1) * Q, :].rearrange("(o n) t -> o n t", o=1)
                                 .broadcast_to([P, Q, T])).then_inc(b_loaded[q], 16)

            def store_x1(s, b, n):
                wait(sp, x1_ready, n + 1)
                sp.sem_inc(sp_passed, 1)
                sp.dma_start(x1[b, bass.ds(s * T, T), :].rearrange("(c p) d -> p c d", p=P), r[:]
                             ).then_inc(x1_stored, 16)

            load_x(0, 0)
            load_x(0, 1)
            move_b(0)

            def tile(s, b):
                n = 2 * s + b
                if not is_first(s, b):
                    store_x1(s if b == 1 else s - 1, 1 - b, n - 1)
                if is_last(s, b):
                    return

                def next_x():
                    if not (isinstance(s, int) and s == S - 1):
                        wait(sp, x_used, n + 1)
                        sp.sem_inc(sp_passed, 1)
                        load_x(s + 1, b)

                move_b(n + 1, next_x)

            for_tiles(sp, tile)
            store_x1(S - 1, 1, 2 * S - 1)
            sp.wait_ge(x1_stored, 16 * 2 * S)

        @block.gpsimd
        def _(pool):
            nc.gpsimd.memset(ident[:], 0.0).then_inc(ident_zero, 1)
            pool.wait_ge(ident_zero, 1)
            nc.gpsimd.affine_select(out=ident[:], in_=ident[:], compare_op=ALU.not_equal, fill=1.0,
                                    base=0, pattern=[[-1, P]], channel_multiplier=1).then_inc(ident_ready, 1)

            def tile(s, b):
                n = 2 * s + b
                for q in range(NQ):
                    pool.wait_ge(b_loaded[q], 16 * n + 16)
                    for g in range(G):
                        i = q * G + g
                        if q == 0:
                            pool.wait_ge(du_done, G * n + g + 1)
                        wait(pool, scanned, Q * (STEPS * n + i - 1))
                        nc.gpsimd.tensor_tensor(
                            drive[:, i % 2], b_all[:, q * Q:(q + 1) * Q, :],
                            du[:, b, g:g + 1, :].broadcast_to([P, Q, T]), ALU.mult
                        ).then_inc(drive_done, 1)

            for_tiles(pool, tile)

        @block.scalar
        def _(act):
            act.wait_ge(weights_in, WEIGHTS)
            nc.scalar.activation(a_neg[:], a_log[:], ACT.Exp).then_inc(a_exp, 1)

            def evacuate(n, i, dst, bias=None):
                act.wait_ge(front_full, NFRONT * n + i + 1)
                rows = dst.shape[0]
                if bias is None:
                    nc.scalar.copy(dst, front[i % FB][:rows, :]).then_inc(front_evac, 1)
                else:
                    nc.scalar.activation(dst, front[i % FB][:rows, :], ACT.Identity, bias=bias
                                         ).then_inc(front_evac, 1)

            def front_part(n, b, i):
                if i == 0:
                    for k in range(KM):
                        evacuate(n, k, xT[:, k, :])
                elif i in PROJ_STEPS:
                    first = 2 * PROJ_STEPS.index(i)
                    if first == G:
                        wait(act, attn_full, 2 * (n - 1))
                    for j in range(first, first + 2):
                        if j < G:
                            if j == 0:
                                wait(act, conv_done, G * n)
                            evacuate(n, KM + j, xh_pad[:, j, NTAP - 1:], b_in[:, j:j + 1])
                        else:
                            evacuate(n, KM + j, zs[:, b, j - G, :], b_in[:, j:j + 1])
                elif i == 8:
                    act.wait_ge(front_evac, NFRONT * n + KM + NPROJ)
                    nc.scalar.activation(zs[:, b], zs[:, b], ACT.Silu).then_inc(gates, 1)
                    act.wait_ge(conv_done, G * n + G)
                    nc.scalar.activation(u[:, b], u[:, b], ACT.Silu).then_inc(gates, 1)
                elif i == 9:
                    evacuate(n, KM + NPROJ, b_rows[:], b_b[:])
                elif 10 <= i < 10 + G:
                    g = i - 10
                    m = g % 2
                    wait(act, delta_done, G * n + g - 1)
                    evacuate(n, KM + NPROJ + 1 + g, dt_raw[:, m], b_dt[:, g:g + 1])
                    act.wait_ge(front_evac, NFRONT * n + KM + NPROJ + 2 + g)
                    nc.scalar.activation(dt_ln[:, m], dt_raw[:, m], ACT.Abs).then_inc(act_chain, 1)
                    act.wait_ge(act_chain, 3 * (G * n + g) + 1)
                    nc.scalar.activation(dt_exp[:, m], dt_ln[:, m], ACT.Exp, scale=-1.0).then_inc(act_chain, 1)
                    act.wait_ge(act_chain, 3 * (G * n + g) + 2)
                    nc.scalar.activation(dt_ln[:, m], dt_exp[:, m], ACT.Ln, bias=1.0).then_inc(act_chain, 1)

            for i in range(STEPS):
                front_part(0, 0, i)

            def tail_part(n, i):
                if i == 7:
                    act.wait_ge(var_ready, n + 1)
                    nc.scalar.activation(rs[:, 1], rs[:, 0], ACT.Ln).then_inc(rs_ln, 1)
                    act.wait_ge(rs_ln, 2 * n + 1)
                    nc.scalar.activation(rs[:, 2], rs[:, 1], ACT.Exp, scale=-0.5).then_inc(rs_ln, 1)

            def tile(s, b):
                n = 2 * s + b
                for q in range(NQ):
                    for g in range(G):
                        i = q * G + g
                        if q == 0:
                            act.wait_ge(delta_done, G * n + g + 1)
                        wait(act, scanned, Q * (STEPS * n + i - 1))
                        if is_first(s, b) and i == 0:
                            act.wait_ge(a_ready, 1)
                        for k in range(Q):
                            st = q * Q + k
                            nc.scalar.activation(decay[:, i % 2, k], delta[:, b, g, :], ACT.Exp,
                                                 scale=a_neg[:, g, st:st + 1]).then_inc(decay_done, 1)
                        if i >= 1 and not is_last(s, b):
                            front_part(n + 1, 1 - b, i - 1)
                        if not is_first(s, b):
                            tail_part(n - 1, i)
                if not is_last(s, b):
                    front_part(n + 1, 1 - b, STEPS - 1)

            for_tiles(act, tile)
            tail_part(2 * S - 1, 7)

        @block.tensor
        def _(pe):
            def free_bank(n, i):
                wait(pe, front_evac, NFRONT * n + i - FB + 1)

            def front_part(n, b, i, s_next):
                if i == 0:
                    pe.wait_ge(x_loaded[b], 16 * s_next + 16)
                    for k in range(KM):
                        free_bank(n, k)
                        for c in range(TB):
                            mm = nc.tensor.transpose(front[k % FB][:, c * P:(c + 1) * P],
                                                     x_tok[:, b, c, k * P:(k + 1) * P], ident[:])
                        mm.then_inc(front_full, 1)
                elif i in PROJ_STEPS:
                    if i == 1:
                        pe.wait_ge(front_evac, NFRONT * n + KM)
                    first = 2 * PROJ_STEPS.index(i)
                    for j in range(first, first + 2):
                        free_bank(n, KM + j)
                        for k in range(KM):
                            mm = nc.tensor.matmul(front[(KM + j) % FB][:], w_in[:, k, j * P:(j + 1) * P],
                                                  xT[:, k, :], start=(k == 0), stop=(k == KM - 1))
                        mm.then_inc(front_full, 1)
                elif i == 9:
                    pe.wait_ge(gates, 2 * n + 2)
                    m = KM + NPROJ
                    free_bank(n, m)
                    wait(pe, b_stored, 16 * n)
                    for k in range(G):
                        mm = nc.tensor.matmul(front[m % FB][:NS, :], w_b[:, k, :], u[:, b, k, :],
                                              start=(k == 0), stop=(k == G - 1))
                    mm.then_inc(front_full, 1)
                elif 10 <= i < 10 + G:
                    g = i - 10
                    m = KM + NPROJ + 1 + g
                    free_bank(n, m)
                    for k in range(G):
                        mm = nc.tensor.matmul(front[m % FB][:], w_dt[:, k, g * P:(g + 1) * P], u[:, b, k, :],
                                              start=(k == 0), stop=(k == G - 1))
                    mm.then_inc(front_full, 1)

            def tail_part(n, b, i):
                if i in (4, 5):
                    half = i - 4
                    pe.wait_ge(y_done, G * n + G)
                    wait(pe, residual, 2 * n + half)
                    for c in range(2):
                        tb = 2 * half + c
                        for k in range(G):
                            mm = nc.tensor.matmul(attn[:, c, :], zs[:, b, k, tb * P:(tb + 1) * P], w_out[:, k, :],
                                                  start=(k == 0), stop=(k == G - 1))
                    mm.then_inc(attn_full, 1)

            pe.wait_ge(weights_in, WEIGHTS)
            pe.wait_ge(ident_ready, 1)
            for i in range(STEPS):
                front_part(0, 0, i, 0)

            def tile(s, b):
                n = 2 * s + b
                for q in range(NQ):
                    for g in range(G):
                        i = q * G + g
                        if not is_last(s, b):
                            front_part(n + 1, 1 - b, i, s + b)
                        pe.wait_ge(scanned, Q * (STEPS * n + i + 1))
                        if q == 0:
                            wait(pe, y_evac, G * (n - 1) + g + 1)
                        for k in range(Q):
                            mm = nc.tensor.matmul(ysum[g][:], ident[:], h[:, i % 2, k, :],
                                                  start=(q == 0 and k == 0), stop=(q == NQ - 1 and k == Q - 1))
                        mm.then_inc(h_summed, 1)
                        if not is_first(s, b):
                            tail_part(n - 1, 1 - b, i)

            for_tiles(pe, tile)
            for i in (4, 5):
                tail_part(2 * S - 1, 1, i)

        @block.vector
        def _(dve):
            dve.wait_ge(weights_in, WEIGHTS)
            dve.wait_ge(a_exp, 1)
            nc.vector.memset(state[:], 0.0).then_inc(saved, 1)
            nc.vector.memset(carry[:], 0.0).then_inc(carried, 1)
            nc.vector.tensor_scalar(a_neg[:], a_neg[:], -1.0, None, ALU.mult).then_inc(a_ready, 1)
            CHAIN = NTAP - 1
            SOFT = 4

            def front_part(n, b, i, chain):
                if i == 3:
                    dve.wait_ge(carried, 2 * n + 1)
                    wait(dve, conv_done, G * n)
                    nc.vector.tensor_copy(xh_pad[:, :, 0:NTAP - 1], carry[:, b]).then_inc(carried, 1)
                if 4 <= i < 4 + G:
                    g = i - 4
                    dve.wait_ge(front_evac, NFRONT * n + KM + g + 1)
                    if g == 0:
                        dve.wait_ge(carried, 2 * n + 2)
                        wait(dve, y_done, G * (n - 1))
                    nc.vector.tensor_scalar(u[:, b, g, :], xh_pad[:, g, 0:T], conv_w[:, g, 0:1], conv_b[:, g:g + 1],
                                            ALU.mult, ALU.add).then_inc(dve_chain, 1)
                    for t in range(1, NTAP):
                        chain[0] += 1
                        dve.wait_ge(dve_chain, chain[0])
                        last = nc.vector.scalar_tensor_tensor(
                            u[:, b, g, :], xh_pad[:, g, t:t + T], conv_w[:, g, t:t + 1], u[:, b, g, :],
                            ALU.mult, ALU.add)
                        last.then_inc(conv_done if t == NTAP - 1 else dve_chain, 1)
                    if g == G - 1:
                        nc.vector.tensor_copy(carry[:, b], xh_pad[:, :, T:T + NTAP - 1]).then_inc(carried, 1)
                if 11 <= i < 11 + G:
                    g = i - 11
                    m = g % 2
                    dve.wait_ge(act_chain, 3 * (G * n + g) + 3)
                    nc.vector.tensor_scalar(dt_tmp[:], dt_exp[:, m], 1.0, None, ALU.add).then_inc(dve_chain, 1)
                    chain[0] += 1
                    dve.wait_ge(dve_chain, chain[0])
                    nc.vector.scalar_tensor_tensor(dt_exp[:, m], dt_tmp[:], -1.0, dt_exp[:, m],
                                                   ALU.add, ALU.subtract).then_inc(dve_chain, 1)
                    nc.vector.scalar_tensor_tensor(dt_ln[:, m], dt_raw[:, m], 0.0, dt_ln[:, m],
                                                   ALU.max, ALU.add).then_inc(dve_chain, 1)
                    chain[0] += 2
                    dve.wait_ge(dve_chain, chain[0])
                    nc.vector.tensor_tensor(delta[:, b, g, :], dt_ln[:, m], dt_exp[:, m], ALU.subtract
                                            ).then_inc(delta_done, 1)
                    dve.wait_ge(delta_done, G * n + g + 1)
                    nc.vector.tensor_tensor(du[:, b, g, :], delta[:, b, g, :], u[:, b, g, :], ALU.mult
                                            ).then_inc(du_done, 1)

            def tail_part(n, b, i, chain):
                if i < G:
                    g = i
                    dve.wait_ge(h_summed, STEPS * n + STEPS)
                    nc.vector.scalar_tensor_tensor(u[:, b, g, :], u[:, b, g, :], d_skip[:, g:g + 1], ysum[g][:],
                                                   ALU.mult, ALU.add).then_inc(y_evac, 1)
                    dve.wait_ge(y_evac, G * n + g + 1)
                    nc.vector.tensor_tensor(zs[:, b, g, :], u[:, b, g, :], zs[:, b, g, :], ALU.mult).then_inc(y_done, 1)
                if i in (5, 6):
                    half = i - 5
                    dve.wait_ge(attn_full, 2 * n + half + 1)
                    dve.wait_ge(x_used, n + 1)
                    part = r[:, 2 * half:2 * half + 2, :]
                    nc.vector.tensor_tensor(part, attn[:], part, ALU.add).then_inc(residual, 1)
                if i == 6:
                    dve.wait_ge(residual, 2 * n + 2)
                    for c in range(TB):
                        nc.vector.bn_stats(stats[:, c], r[:, c]).then_inc(dve_chain, 1)
                    chain[0] += TB
                    dve.wait_ge(dve_chain, chain[0])
                    dve.sem_inc(dve_passed, 1)
                    for c in range(TB):
                        nc.vector.bn_aggr(mv[:, c], stats[:, c]).then_inc(dve_chain, 1)
                    chain[0] += TB
                    dve.wait_ge(dve_chain, chain[0])
                    nc.vector.tensor_scalar(rs[:, 0], mv[:, :, 1], LN_EPS, None, ALU.add).then_inc(var_ready, 1)
                if i == 8:
                    dve.wait_ge(rs_ln, 2 * n + 2)
                    nc.vector.tensor_tensor(rs[:, 1], rs[:, 2], rs[:, 2], ALU.mult).then_inc(dve_chain, 1)
                    chain[0] += 1
                    dve.wait_ge(dve_chain, chain[0])
                    nc.vector.tensor_tensor(rs[:, 1], rs[:, 1], rs[:, 0], ALU.mult).then_inc(dve_chain, 1)
                    chain[0] += 1
                    dve.wait_ge(dve_chain, chain[0])
                    nc.vector.tensor_scalar(rs[:, 1], rs[:, 1], -0.5, 1.5, ALU.mult, ALU.add).then_inc(dve_chain, 1)
                    chain[0] += 1
                    dve.wait_ge(dve_chain, chain[0])
                    nc.vector.tensor_tensor(rs[:, 3], rs[:, 1], rs[:, 2], ALU.mult).then_inc(dve_chain, 1)
                    chain[0] += 1
                    dve.wait_ge(dve_chain, chain[0])
                    for c in range(TB):
                        last = nc.vector.tensor_scalar(r[:, c], r[:, c], mv[:, c, 0:1], rs[:, 3, c:c + 1],
                                                       ALU.subtract, ALU.mult)
                        if c < TB - 1:
                            last.then_inc(dve_chain, 1)
                            chain[0] += 1
                    dve.wait_ge(dve_chain, chain[0])
                    last.then_inc(x1_ready, 1)

            FRONT_LINKS = G * CHAIN + 3 * G
            TAIL_LINKS = 2 * TB + 4 + TB - 1

            chain = [0]
            for i in range(STEPS):
                front_part(0, 0, i, chain)
            assert chain[0] == FRONT_LINKS

            def tile(s, b):
                n = 2 * s + b
                start = FRONT_LINKS * (n + 1) + TAIL_LINKS * (0 if is_first(s, b) else (n - 1))
                chain = [start]
                for q in range(NQ):
                    for g in range(G):
                        i = q * G + g
                        wait(dve, h_summed, STEPS * n + i - 1)
                        if q == 0 and g == 0:
                            dve.wait_ge(saved, 1 + STEPS * (n - 1) if not is_first(s, b) else 1)
                        dve.wait_ge(drive_done, STEPS * n + i + 1)
                        for k in range(Q):
                            st = q * Q + k
                            dve.wait_ge(decay_done, Q * (STEPS * n + i) + k + 1)
                            nc.vector.tensor_tensor_scan(h[:, i % 2, k, :], decay[:, i % 2, k, :],
                                                         drive[:, i % 2, k, :], state[:, b, g, st:st + 1],
                                                         ALU.mult, ALU.add).then_inc(scanned, 1)
                        dve.wait_ge(scanned, Q * (STEPS * n + i + 1))
                        nc.vector.tensor_copy(state[:, b, g, q * Q:(q + 1) * Q], h[:, i % 2, :, T - 1]
                                              ).then_inc(saved, 1)
                        if not is_first(s, b):
                            tail_part(n - 1, 1 - b, i, chain)
                        if not is_last(s, b):
                            front_part(n + 1, 1 - b, i, chain)
                        if i == 11:
                            wait(dve, x1_stored, 16 * n)
                            nc.vector.tensor_tensor(r[:], x_tok[:, b],
                                                    b_out[:].rearrange("p (o d) -> p o d", o=1)
                                                    .broadcast_to([P, TB, DM]), ALU.add).then_inc(x_used, 1)

            for_tiles(dve, tile)
            chain = [FRONT_LINKS * 2 * S + TAIL_LINKS * (2 * S - 1)]
            for i in range(9):
                tail_part(2 * S - 1, 1, i, chain)


def ffn_block(nc, w, x1, out):
    NBATCH, SEQ, DM = x1.shape
    H = w["h1_w"].shape[0]
    KM = DM // P
    KH = H // P
    S = SEQ // T
    NT = NBATCH * S
    SET = 4

    ctx = ExitStack()
    with ctx:
        def sb(name, shape, dt=F32):
            return ctx.enter_context(nc.sbuf_tensor(name, shape, dt))

        def sem(name):
            return ctx.enter_context(nc.semaphore(name))

        w1 = sb("w1", [P, KM, H])
        w2 = sb("w2", [P, KM, H])
        h1 = sb("h1", [P, KH, H])
        h2 = sb("h2", [P, KH, H])
        w3 = sb("w3", [P, KH, DM])
        s1 = sb("s1", [P, KH])
        s2 = sb("s2", [P, KH])
        s_h1 = sb("s_h1", [P, KH])
        s_h2 = sb("s_h2", [P, KH])
        s3 = sb("s3", [P, DM])
        ident = sb("ident2", [P, P])
        stage = sb("stage", [P, 2, H])
        x_tok = sb("x1_tok", [P, 2, TB, DM])
        xT = sb("x1T", [P, KM, T])
        gate = sb("gate", [P, 2, T])
        act_a = sb("act_a", [P, KH, T])
        act_b = sb("act_b", [P, KH, T])
        r = sb("r2", [P, TB, DM])
        stats = sb("stats2", [P, TB, 6])
        mv = sb("mv2", [P, TB, 2])
        rs = sb("rs2", [P, 4, TB])
        bank = [ctx.enter_context(nc.psum_tensor(f"bank{i}", [P, T], F32)) for i in range(2 * SET)]

        scales_in = sem("scales_in")
        ident_zero = sem("ident_zero2")
        ident_ready = sem("ident_ready2")
        stage_in = [sem(f"stage_in{i}") for i in range(2)]
        turned = sem("turned")
        kept = sem("kept")
        x_loaded = [sem(f"x1_loaded{i}") for i in range(2)]
        set_full = sem("set_full")
        act_evac = sem("act_evac")
        dve_evac = sem("dve_evac")
        xT_ready = sem("xT_ready")
        gate_ready = sem("gate_ready")
        gated = sem("gated")
        a1_ready = sem("a1_ready")
        a2_ready = sem("a2_ready")
        o_full = sem("o_full")
        o_scaled = sem("o_scaled")
        chain_sem = sem("ffn_chain")
        var_ready = sem("var_ready2")
        root = sem("root")
        y_ready = sem("y_ready2")
        y_stored = sem("y_stored")
        sp_passed = sem("sp_passed2")
        dve_passed = sem("dve_passed2")

        block = ctx.enter_context(nc.Block())

        pieces = []
        for name, dst, k_blocks in (("w1_w", w1, KM), ("w2_w", w2, KM), ("h1_w", h1, KH), ("h2_w", h2, KH),
                                    ("w3_w", w3, KH)):
            for o in range(w[name].shape[0] // P):
                pieces.append((w[name][o * P:(o + 1) * P, :], dst, k_blocks, o))

        def wait(eng, semaphore, value):
            if not (isinstance(value, int) and value <= 0):
                eng.wait_ge(semaphore, value)

        def for_tiles(eng, body):
            for b in range(2):
                body(0, b)
            with eng.Fori(1, S) as s:
                for b in range(2):
                    body(s, b)

        @block.sync
        def _(sp):
            for dst, src in ((s1, "w1_s"), (s2, "w2_s"), (s_h1, "h1_s"), (s_h2, "h2_s")):
                sp.dma_start(dst[:], w[src].rearrange("(k p) -> p k", p=P),
                             allow_slow_non_contiguous=True).then_inc(scales_in, 16)
            sp.dma_start(s3[:], w["w3_s"].rearrange("(o n) -> o n", o=1).broadcast_to([P, DM])
                         ).then_inc(scales_in, 16)
            done = 0
            before = []
            for m, (src, dst, kb, o) in enumerate(pieces):
                if m >= 2:
                    sp.wait_ge(turned, before[m - 2])
                sp.dma_start(stage[:, m % 2, 0:kb * P], src).then_inc(stage_in[m % 2], 16)
                done += (kb + SET - 1) // SET
                before.append(done)

            def load_x(s, b):
                sp.dma_start(x_tok[:, b], x1[b, bass.ds(s * T, T), :].rearrange("(c p) d -> p c d", p=P)
                             ).then_inc(x_loaded[b], 16)

            load_x(0, 0)
            load_x(0, 1)

            def tile(s, b):
                n = 2 * s + b
                sp.wait_ge(y_ready, n + 1)
                sp.sem_inc(sp_passed, 1)
                sp.dma_start(out[b, bass.ds(s * T, T), :].rearrange("(c p) d -> p c d", p=P), r[:]
                             ).then_inc(y_stored, 16)

            for b in range(2):
                tile(0, b)
                load_x(1, b)
            with sp.Fori(1, S - 1) as s:
                for b in range(2):
                    tile(s, b)
                    load_x(s + 1, b)
            for b in range(2):
                tile(S - 1, b)
            sp.wait_ge(y_stored, 16 * NT)

        @block.gpsimd
        def _(pool):
            nc.gpsimd.memset(ident[:], 0.0).then_inc(ident_zero, 1)
            pool.wait_ge(ident_zero, 1)
            nc.gpsimd.affine_select(out=ident[:], in_=ident[:], compare_op=ALU.not_equal, fill=1.0,
                                    base=0, pattern=[[-1, P]], channel_multiplier=1).then_inc(ident_ready, 1)

        TURNS = sum((kb + SET - 1) // SET for _, _, kb, _ in pieces)

        NSETS = 1 + KH // 2 + 2 + 2 + 1
        assert NSETS % 2 == 0
        DVE_SETS = (*range(1, 1 + KH // 2), NSETS - 1)
        ACT_SETS = (0, *range(1 + KH // 2, NSETS - 1))

        @block.tensor
        def _(pe):
            pe.wait_ge(ident_ready, 1)
            t = 0
            for m, (src, dst, kb, o) in enumerate(pieces):
                pe.wait_ge(stage_in[m % 2], 16 * (m // 2 + 1))
                for k0 in range(0, kb, SET):
                    wait(pe, kept, t + 1 - 2 * SET)
                    width = min(SET, kb - k0)
                    for k in range(width):
                        mm = nc.tensor.transpose(bank[t % (2 * SET)][:, k * P:(k + 1) * P],
                                                 stage[:, m % 2, (k0 + k) * P:(k0 + k + 1) * P], ident[:])
                    mm.then_inc(turned, 1)
                    t += 1
            pe.wait_ge(kept, TURNS)

            def free_set(n, i):
                before, m = (i - 2) % NSETS, n if i >= 2 else n - 1
                for sets, evac in ((ACT_SETS, act_evac), (DVE_SETS, dve_evac)):
                    if before in sets:
                        wait(pe, evac, len(sets) * m + sets.index(before) + 1)

            def banks(i):
                return bank[SET * (i % 2):SET * (i % 2) + SET]

            def tile(s, b):
                n = 2 * s + b
                pe.wait_ge(x_loaded[b], 16 * s + 16)
                free_set(n, 0)
                for k in range(KM):
                    for c in range(TB):
                        mm = nc.tensor.transpose(banks(0)[k][:, c * P:(c + 1) * P],
                                                 x_tok[:, b, c, k * P:(k + 1) * P], ident[:])
                mm.then_inc(set_full, 1)
                i = 1
                pe.wait_ge(xT_ready, KM * n + KM)
                for o in range(0, KH, 2):
                    free_set(n, i)
                    for j, (wt, blk) in enumerate(((w1, o), (w2, o), (w1, o + 1), (w2, o + 1))):
                        for k in range(KM):
                            mm = nc.tensor.matmul(banks(i)[j][:], wt[:, k, blk * P:(blk + 1) * P], xT[:, k, :],
                                                  start=(k == 0), stop=(k == KM - 1))
                    mm.then_inc(set_full, 1)
                    i += 1
                for wt, src, ready in ((h1, act_a, gated), (h2, act_b, a1_ready)):
                    for half in range(2):
                        free_set(n, i)
                        for k in range(KH):
                            if half == 0:
                                pe.wait_ge(ready, KH * n + k + 1)
                            for j in range(SET):
                                o = half * SET + j
                                mm = nc.tensor.matmul(banks(i)[j][:], wt[:, k, o * P:(o + 1) * P], src[:, k, :],
                                                      start=(k == 0), stop=(k == KH - 1))
                        mm.then_inc(set_full, 1)
                        i += 1
                free_set(n, i)
                pe.wait_ge(a2_ready, KH * n + KH)
                for c in range(TB):
                    for k in range(KH):
                        mm = nc.tensor.matmul(banks(i)[c][:, 0:DM], act_a[:, k, c * P:(c + 1) * P], w3[:, k, :],
                                              start=(k == 0), stop=(k == KH - 1))
                mm.then_inc(set_full, 1)

            for_tiles(pe, tile)

        @block.scalar
        def _(act):
            t = 0
            for src, dst, kb, o in pieces:
                for k0 in range(0, kb, SET):
                    width = min(SET, kb - k0)
                    act.wait_ge(turned, t + 1)
                    nc.scalar.copy(dst[:, k0:k0 + width, o * P:(o + 1) * P],
                                   bank[t % (2 * SET)][:, 0:width * P].rearrange("p (k o) -> p k o", k=width)
                                   ).then_inc(kept, 1)
                    t += 1
            act.wait_ge(scales_in, 16 * 5)

            def banks(i):
                return bank[SET * (i % 2):SET * (i % 2) + SET]

            def tile(s, b):
                n = 2 * s + b
                act.wait_ge(set_full, NSETS * n + 1)
                for k in range(KM):
                    nc.scalar.copy(xT[:, k, :], banks(0)[k][:]).then_inc(xT_ready, 1)
                act.wait_ge(xT_ready, KM * n + KM)
                nc.scalar.sem_inc(act_evac, 1)
                i = 1
                for o in range(0, KH, 2):
                    act.wait_ge(set_full, NSETS * n + i + 1)
                    for j in range(2):
                        wait(act, gated, KH * n + o + j - 1)
                        nc.scalar.activation(gate[:, j], banks(i)[2 * j][:], ACT.Silu, scale=s1[:, o + j:o + j + 1]
                                             ).then_inc(gate_ready, 1)
                    i += 1
                for dst, scale, ready in ((act_b, s_h1, a1_ready), (act_a, s_h2, a2_ready)):
                    for half in range(2):
                        act.wait_ge(set_full, NSETS * n + i + 1)
                        if half == 0:
                            pass
                        for j in range(SET):
                            o = half * SET + j
                            last = nc.scalar.activation(dst[:, o, :], banks(i)[j][:], ACT.Gelu,
                                                        scale=scale[:, o:o + 1]).then_inc(ready, 1)
                        act.wait_ge(ready, KH * n + half * SET + SET)
                        nc.scalar.sem_inc(act_evac, 1)
                        i += 1
                act.wait_ge(var_ready, n + 1)
                nc.scalar.activation(rs[:, 1], rs[:, 0], ACT.Sqrt).then_inc(root, 1)

            for_tiles(act, tile)

        @block.vector
        def _(dve):
            dve.wait_ge(scales_in, 16 * 5)

            def banks(i):
                return bank[SET * (i % 2):SET * (i % 2) + SET]

            LINKS = TB + 2 * TB + 1 + TB - 1

            def tile(s, b):
                n = 2 * s + b
                i = 1
                for o in range(0, KH, 2):
                    for j in range(2):
                        dve.wait_ge(gate_ready, KH * n + o + j + 1)
                        dve.wait_ge(set_full, NSETS * n + i + 1)
                        nc.vector.scalar_tensor_tensor(act_a[:, o + j, :], banks(i)[2 * j + 1][:],
                                                       s2[:, o + j:o + j + 1], gate[:, j], ALU.mult, ALU.mult
                                                       ).then_inc(gated, 1)
                    dve.wait_ge(gated, KH * n + o + 2)
                    nc.vector.sem_inc(dve_evac, 1)
                    i += 1
                i += 4
                link = LINKS * n
                dve.wait_ge(set_full, NSETS * n + i + 1)
                wait(dve, y_stored, 16 * n)
                for c in range(TB):
                    nc.vector.tensor_tensor(r[:, c], banks(i)[c][:, 0:DM], s3[:], ALU.mult).then_inc(chain_sem, 1)
                dve.wait_ge(chain_sem, link + TB)
                nc.vector.sem_inc(dve_evac, 1)
                link = link + TB
                nc.vector.tensor_tensor(r[:], r[:], x_tok[:, b], ALU.add).then_inc(o_scaled, 1)
                dve.wait_ge(o_scaled, n + 1)
                for c in range(TB):
                    nc.vector.bn_stats(stats[:, c], r[:, c]).then_inc(chain_sem, 1)
                dve.wait_ge(chain_sem, link + TB)
                dve.sem_inc(dve_passed, 1)
                for c in range(TB):
                    nc.vector.bn_aggr(mv[:, c], stats[:, c]).then_inc(chain_sem, 1)
                dve.wait_ge(chain_sem, link + 2 * TB)
                link = link + 2 * TB
                nc.vector.tensor_scalar(rs[:, 0], mv[:, :, 1], LN_EPS, None, ALU.add).then_inc(var_ready, 1)
                dve.wait_ge(root, n + 1)
                nc.vector.reciprocal(rs[:, 2], rs[:, 1]).then_inc(chain_sem, 1)
                link = link + 1
                dve.wait_ge(chain_sem, link)
                for c in range(TB):
                    last = nc.vector.tensor_scalar(r[:, c], r[:, c], mv[:, c, 0:1], rs[:, 2, c:c + 1],
                                                   ALU.subtract, ALU.mult)
                    if c < TB - 1:
                        last.then_inc(chain_sem, 1)
                dve.wait_ge(chain_sem, link + TB - 1)
                last.then_inc(y_ready, 1)

            for_tiles(dve, tile)


def build(nc, ins, out):
    x = ins["L0_attn_x"]
    NBATCH, SEQ, DM = x.shape
    NS = ins["L0_attn_A_log"].shape[1]
    x1 = nc.dram_tensor("x1_scratch", (NBATCH, SEQ, DM), F32).ap()
    b_scratch = nc.dram_tensor("b_scratch", (NS, T), F32).ap()
    mamba_block(nc, {k[len("L0_attn_"):]: v for k, v in ins.items() if "attn" in k}, x, x1, b_scratch)
    ffn_block(nc, {k[len("L0_ffn_"):]: v for k, v in ins.items() if "ffn" in k}, x1, out)


_OUT = ((2, 4096, 256), "float32")


def kernel(**inputs):
    import numpy as _np
    import concourse.bacc as _bacc
    from concourse import mybir as _mybir
    from concourse.bass_utils import run_bass_kernel_spmd as _run

    nc = _bacc.Bacc("TRN2", target_bir_lowering=False, num_devices=1)
    arrays, ins = {}, {}
    for name in inputs:
        a = _np.ascontiguousarray(inputs[name])
        arrays[f"in_{name}"] = a
        ins[name] = nc.dram_tensor(f"in_{name}", a.shape, _mybir.dt.from_np(a.dtype), kind="ExternalInput").ap()
    out = nc.dram_tensor("out_0", _OUT[0], _mybir.dt.from_np(_np.dtype(_OUT[1])), kind="ExternalOutput").ap()
    build(nc, ins, out)
    r = _run(nc, [arrays], core_ids=[0])
    return r.results[0]["out_0"]
```

```python
from contextlib import ExitStack

import concourse.bass as bass
from concourse import mybir

F32 = mybir.dt.float32
F32R = mybir.dt.float32r
ALU = mybir.AluOpType
ACT = mybir.ActivationFunctionType

P = 128
T = 512
TB = T // P
LN_EPS = 1e-5
EXP_LN = "natural_log_exp_and_others"


def mamba_block(nc, w, x, x1, b_scratch):
    NBATCH, SEQ, DM = x.shape
    DI, NS = w["A_log"].shape
    NTAP = w["conv_w"].shape[2]
    G = DI // P
    KM = DM // P
    Q = 4
    NQ = NS // Q
    STEPS = NQ * G
    S = SEQ // T
    NPROJ = 2 * G
    NFRONT = KM + NPROJ + 1 + G
    FB = 3
    PROJ_STEPS = (1, 2, 6, 7)
    assert NBATCH == 2 and NFRONT % FB == 0 and STEPS == 16 and NPROJ == 2 * len(PROJ_STEPS)

    ctx = ExitStack()
    with ctx:
        def sb(name, shape, dt=F32):
            return ctx.enter_context(nc.sbuf_tensor(name, shape, dt))

        def sem(name):
            return ctx.enter_context(nc.semaphore(name))

        w_in = sb("w_in", [P, KM, 2 * DI])
        w_dt = sb("w_dt", [P, G, DI])
        w_b = sb("w_b", [P, G, NS])
        w_out = sb("w_out", [P, G, DM])
        b_in = sb("b_in", [P, NPROJ])
        conv_w = sb("conv_w", [P, G, NTAP])
        conv_b = sb("conv_b", [P, G])
        b_dt = sb("b_dt", [P, G])
        d_skip = sb("d_skip", [P, G])
        b_b = sb("b_b", [NS, 1])
        b_out = sb("b_out", [P, DM])
        a_log = sb("a_log", [P, G, NS])
        a_neg = sb("a_neg", [P, G, NS])
        ident = sb("ident", [P, P])
        x_tok = sb("x_tok", [P, 2, TB, DM])
        xT = sb("xT", [P, KM, T])
        xh_pad = sb("xh_pad", [P, G, NTAP - 1 + T])
        carry = sb("carry", [P, 2, G, NTAP - 1])
        u = sb("u", [P, 2, G, T])
        zs = sb("zs", [P, 2, G, T])
        dt_raw = sb("dt_raw", [P, 2, T])
        dt_exp = sb("dt_exp", [P, 2, T])
        dt_ln = sb("dt_ln", [P, 2, T])
        dt_tmp = sb("dt_tmp", [P, T])
        delta = sb("delta", [P, 2, G, T])
        du = sb("du", [P, 2, G, T])
        b_rows = sb("b_rows", [NS, T])
        b_all = sb("b_all", [P, NS, T])
        decay = sb("decay", [P, 2, Q, T])
        drive = sb("drive", [P, 2, Q, T])
        h = sb("h", [P, 2, Q, T])
        state = sb("state", [P, 2, G, NS])
        r = sb("r", [P, TB, DM])
        stats = sb("stats", [P, TB, 6])
        mv = sb("mv", [P, TB, 2])
        rs = sb("rs", [P, 4, TB])

        ysum = [ctx.enter_context(nc.psum_tensor(f"ysum{g}", [P, T], F32)) for g in range(G)]
        front = [ctx.enter_context(nc.psum_tensor(f"front{i}", [P, T], F32)) for i in range(FB)]
        attn = ctx.enter_context(nc.psum_tensor("attn", [P, 2, DM], F32))

        weights_in = sem("weights_in")
        ident_zero = sem("ident_zero")
        ident_ready = sem("ident_ready")
        a_ready = sem("a_ready")
        a_exp = sem("a_exp")
        x_loaded = [sem(f"x_loaded{b}") for b in range(2)]
        front_full = sem("front_full")
        front_evac = sem("front_evac")
        conv_done = sem("conv_done")
        carried = sem("carried")
        gates = sem("gates")
        act_chain = sem("act_chain")
        dve_chain = sem("dve_chain")
        delta_done = sem("delta_done")
        du_done = sem("du_done")
        b_stored = sem("b_stored")
        b_loaded = [sem(f"b_loaded{q}") for q in range(NQ)]
        decay_done = sem("decay_done")
        drive_done = sem("drive_done")
        scanned = sem("scanned")
        saved = sem("saved")
        h_summed = sem("h_summed")
        y_done = sem("y_done")
        y_evac = sem("y_evac")
        attn_full = sem("attn_full")
        x_used = sem("x_used")
        residual = sem("residual")
        rs_ln = sem("rs_ln")
        var_ready = sem("var_ready")
        x1_ready = sem("x1_ready")
        x1_stored = sem("x1_stored")
        sp_passed = sem("sp_passed")
        dve_passed = sem("dve_passed")

        block = ctx.enter_context(nc.Block())

        weight_loads = [
            (w_in[:], w["W_in"].rearrange("(k p) n -> p k n", p=P)),
            (w_dt[:], w["W_dt"].rearrange("(k p) n -> p k n", p=P)),
            (w_b[:], w["W_x"].rearrange("(k p) n -> p k n", p=P)[:, :, NS:2 * NS]),
            (w_out[:], w["W_out"].rearrange("(k p) n -> p k n", p=P)),
            (b_in[:], w["b_in"].rearrange("(k p) -> p k", p=P)),
            (conv_w[:], w["conv_w"].rearrange("(k p) o t -> p k (o t)", p=P)),
            (conv_b[:], w["conv_b"].rearrange("(k p) -> p k", p=P)),
            (b_dt[:], w["b_dt"].rearrange("(k p) -> p k", p=P)),
            (d_skip[:], w["D"].rearrange("(k p) -> p k", p=P)),
            (b_b[:], w["b_x"].rearrange("(n o) -> n o", o=1)[NS:2 * NS, :]),
            (b_out[:], w["b_out"].rearrange("(o n) -> o n", o=1).broadcast_to([P, DM])),
            (a_log[:], w["A_log"].rearrange("(k p) n -> p k n", p=P)),
        ]
        WEIGHTS = 16 * len(weight_loads)

        def for_tiles(eng, body):
            for b in range(2):
                body(0, b)
            with eng.Fori(1, S - 1) as s:
                for b in range(2):
                    body(s, b)
            for b in range(2):
                body(S - 1, b)

        def is_first(s, b):
            return isinstance(s, int) and s == 0 and b == 0

        def is_last(s, b):
            return isinstance(s, int) and s == S - 1 and b == 1

        def wait(eng, semaphore, value):
            if not (isinstance(value, int) and value <= 0):
                eng.wait_ge(semaphore, value)

        @block.sync
        def _(sp):
            for dst, src in weight_loads:
                sp.dma_start(dst, src, allow_slow_non_contiguous=True).then_inc(weights_in, 16)

            def load_x(s, b):
                sp.dma_start(x_tok[:, b], x[b, bass.ds(s * T, T), :].rearrange("(c p) d -> p c d", p=P)
                             ).then_inc(x_loaded[b], 16)

            def move_b(n, between=lambda: None):
                for q in range(NQ):
                    wait(sp, b_loaded[q], 16 * n)
                wait(sp, front_evac, NFRONT * n + KM + NPROJ + 1)
                sp.dma_start(b_scratch, b_rows[:]).then_inc(b_stored, 16)
                wait(sp, b_stored, 16 * n + 16)
                sp.sem_inc(sp_passed, 1)
                for q in range(NQ):
                    if q == NQ - 1:
                        between()
                    wait(sp, drive_done, STEPS * (n - 1) + (q + 1) * G)
                    sp.dma_start(b_all[:, q * Q:(q + 1) * Q, :],
                                 b_scratch[q * Q:(q + 1) * Q, :].rearrange("(o n) t -> o n t", o=1)
                                 .broadcast_to([P, Q, T])).then_inc(b_loaded[q], 16)

            def store_x1(s, b, n):
                wait(sp, x1_ready, TB * n + TB)
                sp.sem_inc(sp_passed, 1)
                sp.dma_start(x1[b, bass.ds(s * T, T), :].rearrange("(c p) d -> p c d", p=P), r[:]
                             ).then_inc(x1_stored, 16)

            load_x(0, 0)
            load_x(0, 1)
            move_b(0)

            def tile(s, b):
                n = 2 * s + b
                if not is_first(s, b):
                    store_x1(s if b == 1 else s - 1, 1 - b, n - 1)
                if is_last(s, b):
                    return

                def next_x():
                    if not (isinstance(s, int) and s == S - 1):
                        wait(sp, x_used, n + 1)
                        sp.sem_inc(sp_passed, 1)
                        load_x(s + 1, b)

                move_b(n + 1, next_x)

            for_tiles(sp, tile)
            store_x1(S - 1, 1, 2 * S - 1)
            sp.wait_ge(x1_stored, 16 * 2 * S)

        @block.gpsimd
        def _(pool):
            nc.gpsimd.memset(ident[:], 0.0).then_inc(ident_zero, 1)
            pool.wait_ge(ident_zero, 1)
            nc.gpsimd.affine_select(out=ident[:], in_=ident[:], compare_op=ALU.not_equal, fill=1.0,
                                    base=0, pattern=[[-1, P]], channel_multiplier=1).then_inc(ident_ready, 1)

            def tile(s, b):
                n = 2 * s + b
                for q in range(NQ):
                    pool.wait_ge(b_loaded[q], 16 * n + 16)
                    for g in range(G):
                        i = q * G + g
                        if q == 0:
                            pool.wait_ge(du_done, G * n + g + 1)
                        wait(pool, scanned, Q * (STEPS * n + i - 1))
                        nc.gpsimd.tensor_tensor(
                            drive[:, i % 2], b_all[:, q * Q:(q + 1) * Q, :],
                            du[:, b, g:g + 1, :].broadcast_to([P, Q, T]), ALU.mult
                        ).then_inc(drive_done, 1)

            for_tiles(pool, tile)

        @block.scalar
        def _(act):
            act.wait_ge(weights_in, WEIGHTS)
            act.preload_act_table_set(EXP_LN)
            nc.scalar.activation(a_neg[:], a_log[:], ACT.Exp).then_inc(a_exp, 1)

            def evacuate(n, i, dst, bias=None):
                act.wait_ge(front_full, NFRONT * n + i + 1)
                rows = dst.shape[0]
                if bias is None:
                    nc.scalar.copy(dst, front[i % FB][:rows, :]).then_inc(front_evac, 1)
                else:
                    nc.scalar.activation(dst, front[i % FB][:rows, :], ACT.Identity, bias=bias
                                         ).then_inc(front_evac, 1)

            def front_part(n, b, i):
                if i == 0:
                    for k in range(KM):
                        evacuate(n, k, xT[:, k, :])
                elif i in PROJ_STEPS:
                    first = 2 * PROJ_STEPS.index(i)
                    if first == G:
                        wait(act, attn_full, 2 * (n - 1))
                    for j in range(first, first + 2):
                        if j < G:
                            if j == 0:
                                wait(act, conv_done, G * n)
                            evacuate(n, KM + j, xh_pad[:, j, NTAP - 1:], b_in[:, j:j + 1])
                        else:
                            evacuate(n, KM + j, zs[:, b, j - G, :], b_in[:, j:j + 1])
                elif i == 8:
                    act.wait_ge(front_evac, NFRONT * n + KM + NPROJ)
                    nc.scalar.activation(zs[:, b], zs[:, b], ACT.Silu).then_inc(gates, 1)
                    act.wait_ge(conv_done, G * n + G)
                    nc.scalar.activation(u[:, b], u[:, b], ACT.Silu).then_inc(gates, 1)
                    act.preload_act_table_set(EXP_LN)
                elif i == 9:
                    evacuate(n, KM + NPROJ, b_rows[:], b_b[:])
                elif 10 <= i < 10 + G:
                    g = i - 10
                    m = g % 2
                    wait(act, delta_done, G * n + g - 1)
                    evacuate(n, KM + NPROJ + 1 + g, dt_raw[:, m], b_dt[:, g:g + 1])
                    act.wait_ge(front_evac, NFRONT * n + KM + NPROJ + 2 + g)
                    nc.scalar.activation(dt_ln[:, m], dt_raw[:, m], ACT.Abs).then_inc(act_chain, 1)
                    act.wait_ge(act_chain, 3 * (G * n + g) + 1)
                    nc.scalar.activation(dt_exp[:, m], dt_ln[:, m], ACT.Exp, scale=-1.0).then_inc(act_chain, 1)
                    act.wait_ge(act_chain, 3 * (G * n + g) + 2)
                    nc.scalar.activation(dt_ln[:, m], dt_exp[:, m], ACT.Ln, bias=1.0).then_inc(act_chain, 1)

            for i in range(STEPS):
                front_part(0, 0, i)

            def tail_part(n, i):
                if i == 7:
                    act.wait_ge(var_ready, n + 1)
                    nc.scalar.activation(rs[:, 1], rs[:, 0], ACT.Ln).then_inc(rs_ln, 1)
                    act.wait_ge(rs_ln, 2 * n + 1)
                    nc.scalar.activation(rs[:, 2], rs[:, 1], ACT.Exp, scale=-0.5).then_inc(rs_ln, 1)

            def tile(s, b):
                n = 2 * s + b
                for q in range(NQ):
                    for g in range(G):
                        i = q * G + g
                        if q == 0:
                            act.wait_ge(delta_done, G * n + g + 1)
                        wait(act, scanned, Q * (STEPS * n + i - 1))
                        if is_first(s, b) and i == 0:
                            act.wait_ge(a_ready, 1)
                        for k in range(Q):
                            st = q * Q + k
                            nc.scalar.activation(decay[:, i % 2, k], delta[:, b, g, :], ACT.Exp,
                                                 scale=a_neg[:, g, st:st + 1]).then_inc(decay_done, 1)
                        if i >= 1 and not is_last(s, b):
                            front_part(n + 1, 1 - b, i - 1)
                        if not is_first(s, b):
                            tail_part(n - 1, i)
                if not is_last(s, b):
                    front_part(n + 1, 1 - b, STEPS - 1)

            for_tiles(act, tile)
            tail_part(2 * S - 1, 7)

        @block.tensor
        def _(pe):
            def free_bank(n, i):
                wait(pe, front_evac, NFRONT * n + i - FB + 1)

            def front_part(n, b, i, s_next):
                if i == 0:
                    pe.wait_ge(x_loaded[b], 16 * s_next + 16)
                    for k in range(KM):
                        free_bank(n, k)
                        for c in range(TB):
                            mm = nc.tensor.transpose(front[k % FB][:, c * P:(c + 1) * P],
                                                     x_tok[:, b, c, k * P:(k + 1) * P], ident[:])
                        mm.then_inc(front_full, 1)
                elif i in PROJ_STEPS:
                    if i == 1:
                        pe.wait_ge(front_evac, NFRONT * n + KM)
                    first = 2 * PROJ_STEPS.index(i)
                    for j in range(first, first + 2):
                        free_bank(n, KM + j)
                        for k in range(KM):
                            mm = nc.tensor.matmul(front[(KM + j) % FB][:], w_in[:, k, j * P:(j + 1) * P],
                                                  xT[:, k, :], start=(k == 0), stop=(k == KM - 1))
                        mm.then_inc(front_full, 1)
                elif i == 9:
                    pe.wait_ge(gates, 2 * n + 2)
                    m = KM + NPROJ
                    free_bank(n, m)
                    wait(pe, b_stored, 16 * n)
                    for k in range(G):
                        mm = nc.tensor.matmul(front[m % FB][:NS, :], w_b[:, k, :], u[:, b, k, :],
                                              start=(k == 0), stop=(k == G - 1))
                    mm.then_inc(front_full, 1)
                elif 10 <= i < 10 + G:
                    g = i - 10
                    m = KM + NPROJ + 1 + g
                    free_bank(n, m)
                    for k in range(G):
                        mm = nc.tensor.matmul(front[m % FB][:], w_dt[:, k, g * P:(g + 1) * P], u[:, b, k, :],
                                              start=(k == 0), stop=(k == G - 1))
                    mm.then_inc(front_full, 1)

            def tail_part(n, b, i):
                if i in (4, 5):
                    half = i - 4
                    pe.wait_ge(y_done, G * n + G)
                    wait(pe, residual, 2 * n + half)
                    for c in range(2):
                        tb = 2 * half + c
                        for k in range(G):
                            mm = nc.tensor.matmul(attn[:, c, :], zs[:, b, k, tb * P:(tb + 1) * P], w_out[:, k, :],
                                                  start=(k == 0), stop=(k == G - 1))
                    mm.then_inc(attn_full, 1)

            pe.wait_ge(weights_in, WEIGHTS)
            pe.wait_ge(ident_ready, 1)
            for i in range(STEPS):
                front_part(0, 0, i, 0)

            def tile(s, b):
                n = 2 * s + b
                for q in range(NQ):
                    for g in range(G):
                        i = q * G + g
                        if not is_last(s, b):
                            front_part(n + 1, 1 - b, i, s + b)
                        pe.wait_ge(scanned, Q * (STEPS * n + i + 1))
                        if q == 0:
                            wait(pe, y_evac, G * (n - 1) + g + 1)
                        for k in range(Q):
                            mm = nc.tensor.matmul(ysum[g][:], ident[:], h[:, i % 2, k, :],
                                                  start=(q == 0 and k == 0), stop=(q == NQ - 1 and k == Q - 1))
                        mm.then_inc(h_summed, 1)
                        if not is_first(s, b):
                            tail_part(n - 1, 1 - b, i)

            for_tiles(pe, tile)
            for i in (4, 5):
                tail_part(2 * S - 1, 1, i)

        @block.vector
        def _(dve):
            dve.wait_ge(weights_in, WEIGHTS)
            dve.wait_ge(a_exp, 1)
            nc.vector.memset(state[:], 0.0).then_inc(saved, 1)
            nc.vector.memset(carry[:], 0.0).then_inc(carried, 1)
            nc.vector.tensor_scalar(a_neg[:], a_neg[:], -1.0, None, ALU.mult).then_inc(a_ready, 1)
            CHAIN = NTAP - 1
            SOFT = 4

            def front_part(n, b, i, chain):
                if i == 3:
                    dve.wait_ge(carried, 2 * n + 1)
                    wait(dve, conv_done, G * n)
                    nc.vector.tensor_copy(xh_pad[:, :, 0:NTAP - 1], carry[:, b]).then_inc(carried, 1)
                if 4 <= i < 4 + G:
                    g = i - 4
                    dve.wait_ge(front_evac, NFRONT * n + KM + g + 1)
                    if g == 0:
                        dve.wait_ge(carried, 2 * n + 2)
                        wait(dve, y_done, G * (n - 1))
                    nc.vector.tensor_scalar(u[:, b, g, :], xh_pad[:, g, 0:T], conv_w[:, g, 0:1], conv_b[:, g:g + 1],
                                            ALU.mult, ALU.add).then_inc(dve_chain, 1)
                    for t in range(1, NTAP):
                        chain[0] += 1
                        dve.wait_ge(dve_chain, chain[0])
                        last = nc.vector.scalar_tensor_tensor(
                            u[:, b, g, :], xh_pad[:, g, t:t + T], conv_w[:, g, t:t + 1], u[:, b, g, :],
                            ALU.mult, ALU.add)
                        last.then_inc(conv_done if t == NTAP - 1 else dve_chain, 1)
                    if g == G - 1:
                        nc.vector.tensor_copy(carry[:, b], xh_pad[:, :, T:T + NTAP - 1]).then_inc(carried, 1)
                if 11 <= i < 11 + G:
                    g = i - 11
                    m = g % 2
                    dve.wait_ge(act_chain, 3 * (G * n + g) + 3)
                    nc.vector.tensor_scalar(dt_tmp[:], dt_exp[:, m], 1.0, None, ALU.add).then_inc(dve_chain, 1)
                    chain[0] += 1
                    dve.wait_ge(dve_chain, chain[0])
                    nc.vector.scalar_tensor_tensor(dt_exp[:, m], dt_tmp[:], -1.0, dt_exp[:, m],
                                                   ALU.add, ALU.subtract).then_inc(dve_chain, 1)
                    nc.vector.scalar_tensor_tensor(dt_ln[:, m], dt_raw[:, m], 0.0, dt_ln[:, m],
                                                   ALU.max, ALU.add).then_inc(dve_chain, 1)
                    chain[0] += 2
                    dve.wait_ge(dve_chain, chain[0])
                    nc.vector.tensor_tensor(delta[:, b, g, :], dt_ln[:, m], dt_exp[:, m], ALU.subtract
                                            ).then_inc(delta_done, 1)
                    dve.wait_ge(delta_done, G * n + g + 1)
                    nc.vector.tensor_tensor(du[:, b, g, :], delta[:, b, g, :], u[:, b, g, :], ALU.mult
                                            ).then_inc(du_done, 1)

            def tail_part(n, b, i, chain):
                if i < G:
                    g = i
                    dve.wait_ge(h_summed, STEPS * n + STEPS)
                    nc.vector.scalar_tensor_tensor(u[:, b, g, :], u[:, b, g, :], d_skip[:, g:g + 1], ysum[g][:],
                                                   ALU.mult, ALU.add).then_inc(y_evac, 1)
                    dve.wait_ge(y_evac, G * n + g + 1)
                    nc.vector.tensor_tensor(zs[:, b, g, :], u[:, b, g, :], zs[:, b, g, :], ALU.mult).then_inc(y_done, 1)
                if i in (5, 6):
                    half = i - 5
                    dve.wait_ge(attn_full, 2 * n + half + 1)
                    dve.wait_ge(x_used, n + 1)
                    part = r[:, 2 * half:2 * half + 2, :]
                    nc.vector.tensor_tensor(part, attn[:], part, ALU.add).then_inc(residual, 1)
                if i == 6:
                    dve.wait_ge(residual, 2 * n + 2)
                    for c in range(TB):
                        nc.vector.bn_stats(stats[:, c], r[:, c]).then_inc(dve_chain, 1)
                    chain[0] += TB
                    dve.wait_ge(dve_chain, chain[0])
                    dve.sem_inc(dve_passed, 1)
                    for c in range(TB):
                        nc.vector.bn_aggr(mv[:, c], stats[:, c]).then_inc(dve_chain, 1)
                    chain[0] += TB
                    dve.wait_ge(dve_chain, chain[0])
                    nc.vector.tensor_scalar(rs[:, 0], mv[:, :, 1], LN_EPS, None, ALU.add).then_inc(var_ready, 1)
                if i == 8:
                    dve.wait_ge(rs_ln, 2 * n + 2)
                    nc.vector.tensor_tensor(rs[:, 1], rs[:, 2], rs[:, 2], ALU.mult).then_inc(dve_chain, 1)
                    chain[0] += 1
                    dve.wait_ge(dve_chain, chain[0])
                    nc.vector.tensor_tensor(rs[:, 1], rs[:, 1], rs[:, 0], ALU.mult).then_inc(dve_chain, 1)
                    chain[0] += 1
                    dve.wait_ge(dve_chain, chain[0])
                    nc.vector.tensor_scalar(rs[:, 1], rs[:, 1], -0.5, 1.5, ALU.mult, ALU.add).then_inc(dve_chain, 1)
                    chain[0] += 1
                    dve.wait_ge(dve_chain, chain[0])
                    nc.vector.tensor_tensor(rs[:, 3], rs[:, 1], rs[:, 2], ALU.mult).then_inc(dve_chain, 1)
                    chain[0] += 1
                    dve.wait_ge(dve_chain, chain[0])
                    for c in range(TB):
                        nc.vector.tensor_scalar(r[:, c], r[:, c], mv[:, c, 0:1], rs[:, 3, c:c + 1],
                                                ALU.subtract, ALU.mult).then_inc(x1_ready, 1)

            FRONT_LINKS = G * CHAIN + 3 * G
            TAIL_LINKS = 2 * TB + 4

            chain = [0]
            for i in range(STEPS):
                front_part(0, 0, i, chain)
            assert chain[0] == FRONT_LINKS

            def tile(s, b):
                n = 2 * s + b
                start = FRONT_LINKS * (n + 1) + TAIL_LINKS * (0 if is_first(s, b) else (n - 1))
                chain = [start]
                for q in range(NQ):
                    for g in range(G):
                        i = q * G + g
                        wait(dve, h_summed, STEPS * n + i - 1)
                        if q == 0 and g == 0:
                            dve.wait_ge(saved, 1 + STEPS * (n - 1) if not is_first(s, b) else 1)
                        dve.wait_ge(drive_done, STEPS * n + i + 1)
                        for k in range(Q):
                            st = q * Q + k
                            dve.wait_ge(decay_done, Q * (STEPS * n + i) + k + 1)
                            nc.vector.tensor_tensor_scan(h[:, i % 2, k, :], decay[:, i % 2, k, :],
                                                         drive[:, i % 2, k, :], state[:, b, g, st:st + 1],
                                                         ALU.mult, ALU.add).then_inc(scanned, 1)
                        dve.wait_ge(scanned, Q * (STEPS * n + i + 1))
                        nc.vector.tensor_copy(state[:, b, g, q * Q:(q + 1) * Q], h[:, i % 2, :, T - 1]
                                              ).then_inc(saved, 1)
                        if not is_first(s, b):
                            tail_part(n - 1, 1 - b, i, chain)
                        if not is_last(s, b):
                            front_part(n + 1, 1 - b, i, chain)
                        if i == 11:
                            wait(dve, x1_stored, 16 * n)
                            nc.vector.tensor_tensor(r[:], x_tok[:, b],
                                                    b_out[:].rearrange("p (o d) -> p o d", o=1)
                                                    .broadcast_to([P, TB, DM]), ALU.add).then_inc(x_used, 1)

            for_tiles(dve, tile)
            chain = [FRONT_LINKS * 2 * S + TAIL_LINKS * (2 * S - 1)]
            for i in range(9):
                tail_part(2 * S - 1, 1, i, chain)


def ffn_block(nc, w, x1, out):
    NBATCH, SEQ, DM = x1.shape
    H = w["h1_w"].shape[0]
    KM = DM // P
    KH = H // P
    S = SEQ // T
    NT = NBATCH * S
    SET = 4
    STAGES = 6
    RAW = 4
    HALF = KH // 2
    OUT = HALF + 4
    NSETS = OUT + 1
    assert NSETS % 2 == 1 and HALF == SET and TB == 4 and KM == 2
    shapes = (("w1_w", KM, H), ("w2_w", KM, H), ("h1_w", KH, H), ("h2_w", KH, H), ("w3_w", KH, DM))
    pieces = [(name, o, kb) for name, kb, n_out in shapes for o in range(n_out // P)]
    TURNS = sum((kb + SET - 1) // SET for _, _, kb in pieces)

    ctx = ExitStack()
    with ctx:
        def sb(name, shape, dt=F32, stack=ctx):
            return stack.enter_context(nc.sbuf_tensor(name, shape, dt))

        def sem(name):
            return ctx.enter_context(nc.semaphore(name))

        s1 = sb("s1", [P, KH])
        s2 = sb("s2", [P, KH])
        s_h1 = sb("s_h1", [P, KH])
        s_h2 = sb("s_h2", [P, KH])
        s3 = sb("s3", [P, DM])
        ident = sb("ident2", [P, P])
        ones = sb("ones", [P, 1])
        differ = sb("differ", [P, TURNS])
        differ_all = sb("differ_all", [P, 1])
        flag = sb("flag", [1, 1], mybir.dt.int32)
        x_tok = sb("x1_tok", [P, 2, TB, DM])
        gate = sb("gate", [P, 2, T])
        r = sb("r2", [P, TB, DM])
        stats = sb("stats2", [P, TB, 6])
        mv = sb("mv2", [P, TB, 2])
        rs = sb("rs2", [P, 4, TB])

        def mode_tensors(tag, dt, parts):
            stack = ExitStack()
            with stack:
                m = {name: sb(f"{name}_{tag}", [P, kb, n_out], dt, stack) for name, kb, n_out in shapes}
                with ExitStack() as staging:
                    m["stage"] = sb(f"stage_{tag}", [P, STAGES, H], F32, staging)
                    m["junk"] = sb(f"junk_{tag}", [P, 2, T], F32, staging)
                m["xT"] = sb(f"xT_{tag}", [P, parts, KM, T], dt, stack)
                m["a"] = sb(f"act_a_{tag}", [P, parts, KH, T], dt, stack)
                m["b"] = sb(f"act_b_{tag}", [P, parts, KH, T], dt, stack)
                m["raw"] = sb(f"raw_{tag}", [P, RAW, T], F32, stack)
            return m

        split = mode_tensors("split", F32R, 2)
        whole = mode_tensors("whole", F32, 1)
        bank = [ctx.enter_context(nc.psum_tensor(f"bank{i}", [P, T], F32)) for i in range(2 * SET)]

        scales_in = sem("scales_in")
        ident_zero = sem("ident_zero2")
        ident_ready = sem("ident_ready2")
        ones_ready = sem("ones_ready")
        compared = sem("compared")
        counted = sem("counted")
        count_full = sem("count_full")
        flag_ready = sem("flag_ready")

        class Sems:
            def __init__(self, tag):
                def mode_sem(name):
                    return sem(f"{name}_{tag}")
                self.stage_in = [mode_sem(f"stage_in{i}") for i in range(STAGES)]
                self.turned = mode_sem("turned")
                self.kept = mode_sem("kept")
                self.x_loaded = [mode_sem(f"x1_loaded{i}") for i in range(2)]
                self.set_full = mode_sem("set_full")
                self.x_full = mode_sem("x_full")
                self.act_evac = mode_sem("act_evac")
                self.dve_evac = mode_sem("dve_evac")
                self.xT_high = mode_sem("xT_high")
                self.xT_ready = mode_sem("xT_ready")
                self.gate_ready = mode_sem("gate_ready")
                self.gated = mode_sem("gated")
                self.high = mode_sem("high")
                self.raw = mode_sem("raw")
                self.low = mode_sem("low")
                self.o_scaled = mode_sem("o_scaled")
                self.o_added = mode_sem("o_added")
                self.chain = mode_sem("ffn_chain")
                self.var_ready = mode_sem("var_ready2")
                self.root = mode_sem("root")
                self.y_ready = mode_sem("y_ready2")
                self.y_stored = mode_sem("y_stored")
                self.sp_passed = mode_sem("sp_passed2")
                self.dve_passed = mode_sem("dve_passed2")

        sems_split, sems_whole = Sems("split"), Sems("whole")
        block = ctx.enter_context(nc.Block())

        def wait(eng, semaphore, value):
            if not (isinstance(value, int) and value <= 0):
                eng.wait_ge(semaphore, value)

        def for_tiles(eng, body):
            for b in range(2):
                body(0, b)
            with eng.Fori(1, S - 1) as s:
                for b in range(2):
                    body(s, b)
            for b in range(2):
                body(S - 1, b)

        def is_last(s, b):
            return isinstance(s, int) and s == S - 1 and b == 1

        def banks(i, b):
            h = (i + b) % 2
            return bank[SET * h:SET * h + SET]

        def by_mode(eng, program):
            eng.wait_ge(flag_ready, 1)
            count = eng.value_load(flag[0:1, 0:1], min_val=0, max_val=1)
            with eng.If(count == 0):
                program(split, sems_split, 2)
            with eng.Else():
                load_weights[eng](whole, sems_whole)
                program(whole, sems_whole, 1)

        def sp_weights(m, q):
            done, after = 0, []
            for i, (name, o, kb) in enumerate(pieces):
                if i >= STAGES:
                    nc.sync.wait_ge(q.turned, after[i - STAGES])
                nc.sync.dma_start(m["stage"][:, i % STAGES, 0:kb * P], w[name][o * P:(o + 1) * P, :]
                                  ).then_inc(q.stage_in[i % STAGES], 16)
                done += (kb + SET - 1) // SET
                after.append(done)

        def pe_weights(m, q):
            t = 0
            for i, (name, o, kb) in enumerate(pieces):
                nc.tensor.wait_ge(q.stage_in[i % STAGES], 16 * (i // STAGES + 1))
                for k0 in range(0, kb, SET):
                    wait(nc.tensor, q.kept, t + 1 - 2 * SET)
                    if q is sems_split:
                        wait(nc.tensor, compared, t + 1 - 2 * SET)
                    for k in range(k0, min(k0 + SET, kb)):
                        mm = nc.tensor.transpose(bank[t % (2 * SET)][:, (k - k0) * P:(k - k0 + 1) * P],
                                                 m["stage"][:, i % STAGES, k * P:(k + 1) * P], ident[:])
                    mm.then_inc(q.turned, 1)
                    t += 1
            nc.tensor.wait_ge(q.kept, TURNS)

        def kept_weights(m):
            t = 0
            for name, o, kb in pieces:
                for k0 in range(0, kb, SET):
                    width = min(SET, kb - k0)
                    yield (t, m[name][:, k0:k0 + width, o * P:(o + 1) * P],
                           bank[t % (2 * SET)][:, 0:width * P].rearrange("p (k o) -> p k o", k=width))
                    t += 1

        def act_weights(m, q):
            for t, kept, turned in kept_weights(m):
                nc.scalar.wait_ge(q.turned, t + 1)
                nc.scalar.copy(kept, turned).then_inc(q.kept, 1)

        def nothing(m, q):
            pass

        load_weights = {nc.sync: sp_weights, nc.tensor: pe_weights, nc.scalar: act_weights, nc.vector: nothing}

        @block.sync
        def _(sp):
            for dst, src in ((s1, "w1_s"), (s2, "w2_s"), (s_h1, "h1_s"), (s_h2, "h2_s")):
                sp.dma_start(dst[:], w[src].rearrange("(k p) -> p k", p=P),
                             allow_slow_non_contiguous=True).then_inc(scales_in, 16)
            sp.dma_start(s3[:], w["w3_s"].rearrange("(o n) -> o n", o=1).broadcast_to([P, DM])
                         ).then_inc(scales_in, 16)
            sp_weights(split, sems_split)

            def program(m, q, parts):
                def load_x(s, b):
                    sp.dma_start(x_tok[:, b], x1[b, bass.ds(s * T, T), :].rearrange("(c p) d -> p c d", p=P)
                                 ).then_inc(q.x_loaded[b], 16)

                def tile(s, b):
                    n = 2 * s + b
                    sp.wait_ge(q.y_ready, TB * n + TB)
                    sp.sem_inc(q.sp_passed, 1)
                    sp.dma_start(out[b, bass.ds(s * T, T), :].rearrange("(c p) d -> p c d", p=P), r[:]
                                 ).then_inc(q.y_stored, 16)
                    if not (isinstance(s, int) and s == S - 1):
                        load_x(s + 1, b)

                load_x(0, 0)
                load_x(0, 1)
                for_tiles(sp, tile)
                sp.wait_ge(q.y_stored, 16 * NT)

            by_mode(sp, program)

        @block.gpsimd
        def _(pool):
            nc.gpsimd.memset(ident[:], 0.0).then_inc(ident_zero, 1)
            pool.wait_ge(ident_zero, 1)
            nc.gpsimd.affine_select(out=ident[:], in_=ident[:], compare_op=ALU.not_equal, fill=1.0,
                                    base=0, pattern=[[-1, P]], channel_multiplier=1).then_inc(ident_ready, 1)

        @block.tensor
        def _(pe):
            pe.wait_ge(ident_ready, 1)
            pe_weights(split, sems_split)
            pe.wait_ge(ones_ready, 1)
            pe.wait_ge(counted, 1)
            nc.tensor.matmul(bank[0][0:1, 0:1], differ_all[:], ones[:], start=True, stop=True
                             ).then_inc(count_full, 1)

            def program(m, q, parts):
                GATE_SETS = range(HALF)

                def free_set(n, i):
                    before, tile = (i - 2, n) if i >= 2 else (i - 2 + NSETS, n - 1)
                    if before in GATE_SETS:
                        wait(pe, q.dve_evac, (HALF + 1) * tile + before + 1)
                    elif before == OUT:
                        wait(pe, q.dve_evac, (HALF + 1) * tile + HALF + 1)
                    else:
                        wait(pe, q.act_evac, 4 * tile + before - HALF + 1)

                def product(dst, lhs, rhs, k, last_k):
                    for v in range(parts):
                        mm = nc.tensor.matmul(dst, lhs(v), rhs(v), start=(k == 0 and v == 0),
                                              stop=(k == last_k and v == parts - 1))
                    return mm

                def turn_x(b, s, target):
                    pe.wait_ge(q.x_loaded[b], 16 * s + 16)
                    for k in range(KM):
                        for c in range(TB):
                            mm = nc.tensor.transpose(target[k][:, c * P:(c + 1) * P],
                                                     x_tok[:, b, c, k * P:(k + 1) * P], ident[:])
                    mm.then_inc(q.x_full, 1)

                if parts == 1:
                    pe.wait_ge(q.kept, TURNS)
                turn_x(0, 0, banks(OUT, 1)[2:4])

                def tile(s, b):
                    n = 2 * s + b
                    pe.wait_ge(q.xT_ready, KM * n + KM)
                    for i in range(HALF):
                        free_set(n, i)
                        for j in range(SET):
                            name, o = ("w1_w", "w2_w")[j % 2], 2 * i + j // 2
                            for k in range(KM):
                                mm = product(banks(i, b)[j][:],
                                             lambda v: m[name][:, k, o * P:(o + 1) * P],
                                             lambda v: m["xT"][:, v, k, :], k, KM - 1)
                        mm.then_inc(q.set_full, 1)
                    for layer, (name, src) in enumerate((("h1_w", "a"), ("h2_w", "b"))):
                        for half in range(2):
                            i = HALF + 2 * layer + half
                            free_set(n, i)
                            for k in range(KH):
                                if half == 0:
                                    block_ready(n, layer, k)
                                for j in range(SET):
                                    o = half * SET + j
                                    mm = product(banks(i, b)[j][:],
                                                 lambda v: m[name][:, k, o * P:(o + 1) * P],
                                                 lambda v: m[src][:, v, k, :], k, KH - 1)
                            mm.then_inc(q.set_full, 1)
                    free_set(n, OUT)
                    if not is_last(s, b):
                        turn_x(1 - b, s + b, banks(OUT, b)[2:4])
                    for k in range(KH):
                        block_ready(n, 2, k)
                        for c in range(TB):
                            for v in range(parts):
                                mm = nc.tensor.matmul(
                                    banks(OUT, b)[c // 2][:, (c % 2) * DM:(c % 2 + 1) * DM],
                                    m["a"][:, v, k, c * P:(c + 1) * P], m["w3_w"][:, k, :],
                                    start=(k == 0 and v == 0 and c % 2 == 0),
                                    stop=(k == KH - 1 and v == parts - 1), skip_group_check=True)
                    mm.then_inc(q.set_full, 1)

                def block_ready(n, layer, k):
                    if parts == 2:
                        pe.wait_ge(q.high, 3 * KH * n + KH * layer + k + 1)
                        pe.wait_ge(q.low, 3 * KH * n + KH * layer + k + 1)
                    elif layer == 0:
                        pe.wait_ge(q.gated, KH * n + k + 1)
                    else:
                        pe.wait_ge(q.raw, 2 * KH * n + KH * (layer - 1) + k + 1)

                for_tiles(pe, tile)

            by_mode(pe, program)

        @block.scalar
        def _(act):
            act_weights(split, sems_split)
            act.wait_ge(scales_in, 16 * 5)

            def program(m, q, parts):
                def tile(s, b):
                    n = 2 * s + b

                    def gate_high(o):
                        act.wait_ge(q.gated, KH * n + o + 1)
                        nc.scalar.copy(m["a"][:, 0, o, :], m["raw"][:, o % RAW, :]).then_inc(q.high, 1)

                    for i in range(HALF):
                        act.wait_ge(q.set_full, NSETS * n + i + 1)
                        for j in range(2):
                            o = 2 * i + j
                            wait(act, q.gated, KH * n + o - 1)
                            nc.scalar.activation(gate[:, j], banks(i, b)[2 * j][:], ACT.Silu,
                                                 scale=s1[:, o:o + 1]).then_inc(q.gate_ready, 1)
                        if parts == 2 and i > 0:
                            for j in range(2):
                                gate_high(2 * i - 2 + j)
                    if parts == 2:
                        for o in range(KH - 2, KH):
                            gate_high(o)
                    for layer, (dst, scale) in enumerate((("b", s_h1), ("a", s_h2))):
                        for half in range(2):
                            i = HALF + 2 * layer + half
                            act.wait_ge(q.set_full, NSETS * n + i + 1)
                            for j in range(SET):
                                o = half * SET + j
                                src = banks(i, b)[j][:]
                                if parts == 1:
                                    nc.scalar.activation(m[dst][:, 0, o, :], src, ACT.Gelu,
                                                         scale=scale[:, o:o + 1]).then_inc(q.raw, 1)
                                    continue
                                wait(act, q.low, 3 * KH * n + KH * (layer + 1) + o - RAW + 1)
                                nc.scalar.activation(m["raw"][:, o % RAW, :], src, ACT.Gelu,
                                                     scale=scale[:, o:o + 1]).then_inc(q.raw, 1)
                                nc.scalar.activation(m[dst][:, 0, o, :], src, ACT.Gelu,
                                                     scale=scale[:, o:o + 1]).then_inc(q.high, 1)
                            if parts == 2:
                                act.wait_ge(q.high, 3 * KH * n + KH * (layer + 1) + half * SET + SET)
                            act.wait_ge(q.raw, 2 * KH * n + KH * layer + half * SET + SET)
                            act.sem_inc(q.act_evac, 1)
                    act.wait_ge(q.var_ready, n + 1)
                    nc.scalar.activation(rs[:, 1], rs[:, 0], ACT.Sqrt).then_inc(q.root, 1)

                for_tiles(act, tile)

            by_mode(act, program)

        @block.vector
        def _(dve):
            nc.vector.memset(ones[:], 1.0).then_inc(ones_ready, 1)
            for t, kept, turned in kept_weights(split):
                dve.wait_ge(sems_split.kept, t + 1)
                wait(dve, compared, t - 1)
                kb = kept.shape[1]
                nc.vector.scalar_tensor_tensor(
                    split["junk"][:, t % 2, 0:kb * P].rearrange("p (k o) -> p k o", k=kb), turned, 0.0,
                    kept.bitcast(F32), ALU.add, ALU.not_equal, accum_out=differ[:, t:t + 1]
                ).then_inc(compared, 1)
            dve.wait_ge(compared, TURNS)
            nc.vector.reduce_sum(differ_all[:], differ[:], mybir.AxisListType.X).then_inc(counted, 1)
            dve.wait_ge(count_full, 1)
            nc.vector.tensor_scalar(flag[:], bank[0][0:1, 0:1], 0.0, None, ALU.not_equal).then_inc(flag_ready, 1)
            dve.wait_ge(scales_in, 16 * 5)

            def program(m, q, parts):
                LINKS = 2 * TB + 1

                def x_parts(n, target):
                    dve.wait_ge(q.x_full, n + 1)
                    wait(dve, q.set_full, NSETS * (n - 1) + HALF)
                    for k in range(KM):
                        nc.vector.tensor_copy(m["xT"][:, 0, k, :], target[k][:]
                                              ).then_inc(q.xT_high if parts == 2 else q.xT_ready, 1)
                    if parts == 2:
                        for k in range(KM):
                            dve.wait_ge(q.xT_high, KM * n + k + 1)
                            nc.vector.tensor_tensor(m["xT"][:, 1, k, :], target[k][:],
                                                    m["xT"][:, 0, k, :].bitcast(F32), ALU.subtract
                                                    ).then_inc(q.xT_ready, 1)

                x_parts(0, banks(OUT, 1)[2:4])

                def low(n, layer, o, dst):
                    nc.vector.tensor_tensor(dst[:, 1, o, :], m["raw"][:, o % RAW, :],
                                            dst[:, 0, o, :].bitcast(F32), ALU.subtract).then_inc(q.low, 1)

                def tile(s, b):
                    n = 2 * s + b

                    def gate_low(o):
                        dve.wait_ge(q.high, 3 * KH * n + o + 1)
                        low(n, 0, o, m["a"])

                    for i in range(HALF):
                        dve.wait_ge(q.set_full, NSETS * n + i + 1)
                        for j in range(2):
                            o = 2 * i + j
                            dve.wait_ge(q.gate_ready, KH * n + o + 1)
                            if parts == 2:
                                wait(dve, q.low, 3 * KH * n + o - RAW + 1)
                            dst = m["raw"][:, o % RAW, :] if parts == 2 else m["a"][:, 0, o, :]
                            nc.vector.scalar_tensor_tensor(dst, banks(i, b)[2 * j + 1][:], s2[:, o:o + 1],
                                                           gate[:, j], ALU.mult, ALU.mult).then_inc(q.gated, 1)
                        dve.wait_ge(q.gated, KH * n + 2 * i + 2)
                        dve.sem_inc(q.dve_evac, 1)
                        if parts == 2 and i > 0:
                            for j in range(2):
                                gate_low(2 * i - 2 + j)
                    if parts == 2:
                        for o in range(KH - 2, KH):
                            gate_low(o)
                        for layer, dst in ((1, "b"), (2, "a")):
                            for o in range(KH):
                                if layer == 2 and o == SET and not is_last(s, b):
                                    x_parts(n + 1, banks(OUT, b)[2:4])
                                dve.wait_ge(q.raw, 2 * KH * n + KH * (layer - 1) + o + 1)
                                dve.wait_ge(q.high, 3 * KH * n + KH * layer + o + 1)
                                low(n, layer, o, m[dst])
                    elif not is_last(s, b):
                        x_parts(n + 1, banks(OUT, b)[2:4])
                    link = LINKS * n
                    dve.wait_ge(q.set_full, NSETS * n + OUT + 1)
                    wait(dve, q.y_stored, 16 * n)
                    for c in range(0, TB, 2):
                        nc.vector.tensor_tensor(
                            r[:, c:c + 2], banks(OUT, b)[c // 2][:].rearrange("p (c d) -> p c d", c=2),
                            s3[:].rearrange("p (o d) -> p o d", o=1).broadcast_to([P, 2, DM]), ALU.mult
                        ).then_inc(q.o_scaled, 1)
                    dve.wait_ge(q.o_scaled, TB // 2 * n + TB // 2)
                    if not is_last(s, b):
                        dve.wait_ge(q.xT_ready, KM * n + 2 * KM)
                    dve.sem_inc(q.dve_evac, 1)
                    nc.vector.tensor_tensor(r[:], r[:], x_tok[:, b], ALU.add).then_inc(q.o_added, 1)
                    dve.wait_ge(q.o_added, n + 1)
                    for c in range(TB):
                        nc.vector.bn_stats(stats[:, c], r[:, c]).then_inc(q.chain, 1)
                    dve.wait_ge(q.chain, link + TB)
                    dve.sem_inc(q.dve_passed, 1)
                    for c in range(TB):
                        nc.vector.bn_aggr(mv[:, c], stats[:, c]).then_inc(q.chain, 1)
                    dve.wait_ge(q.chain, link + 2 * TB)
                    link = link + 2 * TB
                    nc.vector.tensor_scalar(rs[:, 0], mv[:, :, 1], LN_EPS, None, ALU.add).then_inc(q.var_ready, 1)
                    dve.wait_ge(q.root, n + 1)
                    nc.vector.reciprocal(rs[:, 2], rs[:, 1]).then_inc(q.chain, 1)
                    link = link + 1
                    dve.wait_ge(q.chain, link)
                    for c in range(TB):
                        nc.vector.tensor_scalar(r[:, c], r[:, c], mv[:, c, 0:1], rs[:, 2, c:c + 1],
                                                ALU.subtract, ALU.mult).then_inc(q.y_ready, 1)

                for_tiles(dve, tile)

            by_mode(dve, program)


def build(nc, ins, out):
    x = ins["L0_attn_x"]
    NBATCH, SEQ, DM = x.shape
    NS = ins["L0_attn_A_log"].shape[1]
    x1 = nc.dram_tensor("x1_scratch", (NBATCH, SEQ, DM), F32).ap()
    b_scratch = nc.dram_tensor("b_scratch", (NS, T), F32).ap()
    mamba_block(nc, {k[len("L0_attn_"):]: v for k, v in ins.items() if "attn" in k}, x, x1, b_scratch)
    ffn_block(nc, {k[len("L0_ffn_"):]: v for k, v in ins.items() if "ffn" in k}, x1, out)


_OUT = ((2, 4096, 256), "float32")


def kernel(**inputs):
    import numpy as _np
    import concourse.bacc as _bacc
    from concourse import mybir as _mybir
    from concourse.bass_utils import run_bass_kernel_spmd as _run

    nc = _bacc.Bacc("TRN2", target_bir_lowering=False, num_devices=1)
    arrays, ins = {}, {}
    for name in inputs:
        a = _np.ascontiguousarray(inputs[name])
        arrays[f"in_{name}"] = a
        ins[name] = nc.dram_tensor(f"in_{name}", a.shape, _mybir.dt.from_np(a.dtype), kind="ExternalInput").ap()
    out = nc.dram_tensor("out_0", _OUT[0], _mybir.dt.from_np(_np.dtype(_OUT[1])), kind="ExternalOutput").ap()
    build(nc, ins, out)
    r = _run(nc, [arrays], core_ids=[0])
    return r.results[0]["out_0"]
```

```python
from contextlib import ExitStack

import concourse.bass as bass
from concourse import mybir

F32 = mybir.dt.float32
F32R = mybir.dt.float32r
ALU = mybir.AluOpType
ACT = mybir.ActivationFunctionType

P = 128
T = 512
TB = T // P
LN_EPS = 1e-5
EXP_LN = "natural_log_exp_and_others"


def mamba_block(nc, w, x, x1, b_scratch):
    NBATCH, SEQ, DM = x.shape
    DI, NS = w["A_log"].shape
    NTAP = w["conv_w"].shape[2]
    G = DI // P
    KM = DM // P
    Q = 4
    NQ = NS // Q
    STEPS = NQ * G
    S = SEQ // T
    NPROJ = 2 * G
    NFRONT = KM + NPROJ + 1 + G
    FB = 3
    HALVED = (1, 3, 5, 7, 9, 11, 12, 14)
    PROJ_STEPS = (1, 2, 7, 8)
    TAP_STEP = 3
    CONV_STEP = 4
    SILU_STEP = 8
    B_STEP = 9
    DT_STEP = 11
    Y_GROUPS = 2
    OUT_STEPS = (2, 5)
    RES_STEPS = (4, 7)
    NORM_STEP = 8
    ROOT_STEP = 9
    SCALE_STEP = 10
    X_STEP = 11
    assert NBATCH == 2 and NFRONT % FB == 0 and STEPS == 16 and len(HALVED) % 2 == 0
    assert NPROJ == 2 * len(PROJ_STEPS)

    ctx = ExitStack()
    with ctx:
        def sb(name, shape, dt=F32):
            return ctx.enter_context(nc.sbuf_tensor(name, shape, dt))

        def sem(name):
            return ctx.enter_context(nc.semaphore(name))

        w_in = sb("w_in", [P, KM, 2 * DI])
        w_dt = sb("w_dt", [P, G, DI])
        w_b = sb("w_b", [P, G, NS])
        w_out = sb("w_out", [P, G, DM])
        b_in = sb("b_in", [P, NPROJ])
        conv_w = sb("conv_w", [P, G, NTAP])
        conv_b = sb("conv_b", [P, G])
        b_dt = sb("b_dt", [P, G])
        d_skip = sb("d_skip", [P, G])
        b_b = sb("b_b", [NS, 1])
        b_out = sb("b_out", [P, DM])
        a_log = sb("a_log", [P, G, NS])
        a_neg = sb("a_neg", [P, G, NS])
        ident = sb("ident", [P, P])
        x_tok = sb("x_tok", [P, 2, TB, DM])
        xT = sb("xT", [P, KM, T])
        xh_pad = sb("xh_pad", [P, G, NTAP - 1 + T])
        carry = sb("carry", [P, 2, G, NTAP - 1])
        u = sb("u", [P, 2, G, T])
        zs = sb("zs", [P, 2, G, T])
        dt_raw = sb("dt_raw", [P, T])
        dt_exp = sb("dt_exp", [P, T])
        dt_ln = sb("dt_ln", [P, T])
        dt_tmp = sb("dt_tmp", [P, T])
        delta = sb("delta", [P, 2, G, T])
        du = sb("du", [P, 2, G, T])
        b_rows = xT[0:NS, 0, :]
        b_all = sb("b_all", [P, NS, T])
        decay = sb("decay", [P, 2, Q, T])
        drive = sb("drive", [P, 2, Q, T])
        h = sb("h", [P, 2, Q, T])
        pairs = sb("pairs", [P, 2, Q // 2, T])
        state = sb("state", [P, 2, G, NS])
        r = sb("r", [P, TB, DM])
        stats = sb("stats", [P, TB, 6])
        mv = sb("mv", [P, TB, 2])
        rs = sb("rs", [P, 4, TB])

        ysum = [ctx.enter_context(nc.psum_tensor(f"ysum{g}", [P, T], F32)) for g in range(G)]
        front = [ctx.enter_context(nc.psum_tensor(f"front{i}", [P, T], F32)) for i in range(FB)]
        attn = ctx.enter_context(nc.psum_tensor("attn", [P, 2, DM], F32))

        weights_in = sem("weights_in")
        ident_zero = sem("ident_zero")
        ident_ready = sem("ident_ready")
        a_ready = sem("a_ready")
        a_exp = sem("a_exp")
        x_loaded = [sem(f"x_loaded{b}") for b in range(2)]
        front_full = sem("front_full")
        front_evac = sem("front_evac")
        first_tap = sem("first_tap")
        conv_done = sem("conv_done")
        carried = sem("carried")
        u_gated = sem("u_gated")
        z_gated = sem("z_gated")
        act_chain = sem("act_chain")
        dve_chain = sem("dve_chain")
        delta_done = sem("delta_done")
        du_done = sem("du_done")
        b_stored = sem("b_stored")
        b_loaded = [sem(f"b_loaded{q}") for q in range(NQ)]
        decay_done = sem("decay_done")
        drive_done = sem("drive_done")
        scanned = sem("scanned")
        saved = sem("saved")
        h_summed = sem("h_summed")
        halved = sem("halved")
        y_done = sem("y_done")
        y_evac = sem("y_evac")
        attn_full = sem("attn_full")
        x_used = sem("x_used")
        residual = sem("residual")
        rs_ln = sem("rs_ln")
        var_ready = sem("var_ready")
        x1_ready = sem("x1_ready")
        x1_stored = sem("x1_stored")
        sp_passed = sem("sp_passed")
        dve_passed = sem("dve_passed")

        SOFT = 4

        block = ctx.enter_context(nc.Block())

        weight_loads = [
            (w_in[:], w["W_in"].rearrange("(k p) n -> p k n", p=P)),
            (w_dt[:], w["W_dt"].rearrange("(k p) n -> p k n", p=P)),
            (w_b[:], w["W_x"].rearrange("(k p) n -> p k n", p=P)[:, :, NS:2 * NS]),
            (w_out[:], w["W_out"].rearrange("(k p) n -> p k n", p=P)),
            (b_in[:], w["b_in"].rearrange("(k p) -> p k", p=P)),
            (conv_w[:], w["conv_w"].rearrange("(k p) o t -> p k (o t)", p=P)),
            (conv_b[:], w["conv_b"].rearrange("(k p) -> p k", p=P)),
            (b_dt[:], w["b_dt"].rearrange("(k p) -> p k", p=P)),
            (d_skip[:], w["D"].rearrange("(k p) -> p k", p=P)),
            (b_b[:], w["b_x"].rearrange("(n o) -> n o", o=1)[NS:2 * NS, :]),
            (b_out[:], w["b_out"].rearrange("(o n) -> o n", o=1).broadcast_to([P, DM])),
            (a_log[:], w["A_log"].rearrange("(k p) n -> p k n", p=P)),
        ]
        WEIGHTS = 16 * len(weight_loads)

        def for_tiles(eng, body):
            for b in range(2):
                body(0, b)
            with eng.Fori(1, S - 1) as s:
                for b in range(2):
                    body(s, b)
            for b in range(2):
                body(S - 1, b)

        def is_first(s, b):
            return isinstance(s, int) and s == 0 and b == 0

        def halved_count(n, i):
            return len(HALVED) * n + HALVED.index(i) + 1

        def is_last(s, b):
            return isinstance(s, int) and s == S - 1 and b == 1

        def wait(eng, semaphore, value):
            if not (isinstance(value, int) and value <= 0):
                eng.wait_ge(semaphore, value)

        @block.sync
        def _(sp):
            for dst, src in weight_loads:
                sp.dma_start(dst, src, allow_slow_non_contiguous=True).then_inc(weights_in, 16)

            def load_x(s, b):
                sp.dma_start(x_tok[:, b], x[b, bass.ds(s * T, T), :].rearrange("(c p) d -> p c d", p=P)
                             ).then_inc(x_loaded[b], 16)

            def move_b(n, between=lambda: None):
                for q in range(NQ):
                    wait(sp, b_loaded[q], 16 * n)
                wait(sp, front_evac, NFRONT * n + KM + NPROJ + 1)
                sp.dma_start(b_scratch, b_rows).then_inc(b_stored, 16)
                wait(sp, b_stored, 16 * n + 16)
                sp.sem_inc(sp_passed, 1)
                for q in range(NQ):
                    if q == NQ - 1:
                        between()
                    wait(sp, drive_done, 2 * (STEPS * (n - 1) + (q + 1) * G))
                    sp.dma_start(b_all[:, q * Q:(q + 1) * Q, :],
                                 b_scratch[q * Q:(q + 1) * Q, :].rearrange("(o n) t -> o n t", o=1)
                                 .broadcast_to([P, Q, T])).then_inc(b_loaded[q], 16)

            def store_x1(s, b, n):
                wait(sp, x1_ready, TB * n + TB)
                sp.sem_inc(sp_passed, 1)
                sp.dma_start(x1[b, bass.ds(s * T, T), :].rearrange("(c p) d -> p c d", p=P), r[:]
                             ).then_inc(x1_stored, 16)

            load_x(0, 0)
            load_x(0, 1)
            move_b(0)

            def tile(s, b):
                n = 2 * s + b
                if not is_first(s, b):
                    store_x1(s if b == 1 else s - 1, 1 - b, n - 1)
                if is_last(s, b):
                    return

                def next_x():
                    if not (isinstance(s, int) and s == S - 1):
                        wait(sp, x_used, n + 1)
                        sp.sem_inc(sp_passed, 1)
                        load_x(s + 1, b)

                move_b(n + 1, next_x)

            for_tiles(sp, tile)
            store_x1(S - 1, 1, 2 * S - 1)
            sp.wait_ge(x1_stored, 16 * 2 * S)

        @block.gpsimd
        def _(pool):
            nc.gpsimd.memset(ident[:], 0.0).then_inc(ident_zero, 1)
            pool.wait_ge(ident_zero, 1)
            nc.gpsimd.affine_select(out=ident[:], in_=ident[:], compare_op=ALU.not_equal, fill=1.0,
                                    base=0, pattern=[[-1, P]], channel_multiplier=1).then_inc(ident_ready, 1)

            def tile(s, b):
                n = 2 * s + b
                for q in range(NQ):
                    pool.wait_ge(b_loaded[q], 16 * n + 16)
                    for g in range(G):
                        i = q * G + g
                        if q == 0:
                            pool.wait_ge(du_done, G * n + g + 1)
                        for k in range(0, Q, 2):
                            wait(pool, scanned, Q * (STEPS * n + i - 2) + k + 2)
                            nc.gpsimd.tensor_tensor(
                                drive[:, i % 2, k:k + 2], b_all[:, q * Q + k:q * Q + k + 2, :],
                                du[:, b, g:g + 1, :].broadcast_to([P, 2, T]), ALU.mult
                            ).then_inc(drive_done, 1)

            for_tiles(pool, tile)

        @block.scalar
        def _(act):
            act.wait_ge(weights_in, WEIGHTS)
            act.preload_act_table_set(EXP_LN)
            nc.scalar.activation(a_neg[:], a_log[:], ACT.Exp).then_inc(a_exp, 1)

            def evacuate(n, i, dst, bias=None):
                act.wait_ge(front_full, NFRONT * n + i + 1)
                rows = dst.shape[0]
                if bias is None:
                    nc.scalar.copy(dst, front[i % FB][:rows, :]).then_inc(front_evac, 1)
                else:
                    nc.scalar.activation(dst, front[i % FB][:rows, :], ACT.Identity, bias=bias
                                         ).then_inc(front_evac, 1)

            def gate_z(n, b):
                act.wait_ge(front_evac, NFRONT * n + KM + NPROJ)
                nc.scalar.activation(zs[:, b], zs[:, b], ACT.Silu).then_inc(z_gated, 1)

            def front_part(n, b, i, half):
                if i == 0:
                    wait(act, b_stored, 16 * n)
                    evacuate(n, half, xT[:, half, :])
                elif i in PROJ_STEPS:
                    first = 2 * PROJ_STEPS.index(i)
                    if first == G:
                        wait(act, attn_full, 2 * (n - 1))
                    j = first + half
                    if j < G:
                        if j == 0:
                            wait(act, conv_done, G * n)
                        evacuate(n, KM + j, xh_pad[:, j, NTAP - 1:], b_in[:, j:j + 1])
                    else:
                        evacuate(n, KM + j, zs[:, b, j - G, :], b_in[:, j:j + 1])
                elif i in (TAP_STEP, TAP_STEP + 1):
                    g = 2 * (i - TAP_STEP) + half
                    act.wait_ge(front_evac, NFRONT * n + KM + g + 1)
                    act.wait_ge(carried, 2 * n + 2)
                    wait(act, y_done, G * (n - 1))
                    nc.scalar.activation(u[:, b, g, :], xh_pad[:, g, 0:T], ACT.Identity,
                                         bias=conv_b[:, g:g + 1], scale=conv_w[:, g, 0:1]
                                         ).then_inc(first_tap, 1)
                if i == SILU_STEP and half == 1:
                    act.wait_ge(conv_done, G * n + G)
                    nc.scalar.activation(u[:, b], u[:, b], ACT.Silu).then_inc(u_gated, 1)
                    if not (isinstance(n, int) and n == 0):
                        gate_z(n - 1, 1 - b)
                    act.preload_act_table_set(EXP_LN)
                elif i == B_STEP and half == 1:
                    evacuate(n, KM + NPROJ, b_rows, b_b[:])
                elif DT_STEP <= i < DT_STEP + G and half == 1:
                    g = i - DT_STEP
                    wait(act, delta_done, G * n + g)
                    evacuate(n, KM + NPROJ + 1 + g, dt_raw[:], b_dt[:, g:g + 1])
                    act.wait_ge(front_evac, NFRONT * n + KM + NPROJ + 2 + g)
                    link = SOFT * (G * n + g)
                    nc.scalar.activation(dt_ln[:], dt_raw[:], ACT.Abs).then_inc(act_chain, 1)
                    act.wait_ge(act_chain, link + 1)
                    nc.scalar.activation(dt_exp[:], dt_ln[:], ACT.Exp, scale=-1.0).then_inc(act_chain, 1)
                    act.wait_ge(act_chain, link + 2)
                    nc.scalar.activation(dt_tmp[:], dt_exp[:], ACT.Identity, bias=1.0).then_inc(act_chain, 1)
                    nc.scalar.activation(dt_ln[:], dt_exp[:], ACT.Ln, bias=1.0).then_inc(act_chain, 1)

            for i in range(STEPS):
                for half in range(2):
                    front_part(0, 0, i, half)

            def tail_part(n, i):
                if i == ROOT_STEP:
                    act.wait_ge(var_ready, n + 1)
                    nc.scalar.activation(rs[:, 1], rs[:, 0], ACT.Ln).then_inc(rs_ln, 1)
                    act.wait_ge(rs_ln, 2 * n + 1)
                    nc.scalar.activation(rs[:, 2], rs[:, 1], ACT.Exp, scale=-0.5).then_inc(rs_ln, 1)

            def tile(s, b):
                n = 2 * s + b
                for q in range(NQ):
                    for g in range(G):
                        i = q * G + g
                        if q == 0:
                            act.wait_ge(delta_done, G * n + g + 1)
                        wait(act, scanned, Q * (STEPS * n + i - 1))
                        if is_first(s, b) and i == 0:
                            act.wait_ge(a_ready, 1)
                        for k in range(Q):
                            st = q * Q + k
                            nc.scalar.activation(decay[:, i % 2, k], delta[:, b, g, :], ACT.Exp,
                                                 scale=a_neg[:, g, st:st + 1]).then_inc(decay_done, 1)
                            if k % 2 == 1 and i >= 1 and not is_last(s, b):
                                front_part(n + 1, 1 - b, i - 1, k // 2)
                        if is_last(s, b) and i == SILU_STEP + 1:
                            gate_z(n, b)
                            act.preload_act_table_set(EXP_LN)
                        if not is_first(s, b):
                            tail_part(n - 1, i)
                if not is_last(s, b):
                    for half in range(2):
                        front_part(n + 1, 1 - b, STEPS - 1, half)

            for_tiles(act, tile)
            tail_part(2 * S - 1, ROOT_STEP)

        @block.tensor
        def _(pe):
            def free_bank(n, i):
                wait(pe, front_evac, NFRONT * n + i - FB + 1)

            def front_part(n, b, i, s_next):
                if i == 0:
                    pe.wait_ge(x_loaded[b], 16 * s_next + 16)
                    for k in range(KM):
                        free_bank(n, k)
                        for c in range(TB):
                            mm = nc.tensor.transpose(front[k % FB][:, c * P:(c + 1) * P],
                                                     x_tok[:, b, c, k * P:(k + 1) * P], ident[:])
                        mm.then_inc(front_full, 1)
                elif i in PROJ_STEPS:
                    if i == 1:
                        pe.wait_ge(front_evac, NFRONT * n + KM)
                    first = 2 * PROJ_STEPS.index(i)
                    for j in range(first, first + 2):
                        free_bank(n, KM + j)
                        for k in range(KM):
                            mm = nc.tensor.matmul(front[(KM + j) % FB][:], w_in[:, k, j * P:(j + 1) * P],
                                                  xT[:, k, :], start=(k == 0), stop=(k == KM - 1))
                        mm.then_inc(front_full, 1)
                elif i == B_STEP:
                    pe.wait_ge(u_gated, n + 1)
                    m = KM + NPROJ
                    free_bank(n, m)
                    for k in range(G):
                        mm = nc.tensor.matmul(front[m % FB][:NS, :], w_b[:, k, :], u[:, b, k, :],
                                              start=(k == 0), stop=(k == G - 1))
                    mm.then_inc(front_full, 1)
                elif DT_STEP <= i < DT_STEP + G:
                    g = i - DT_STEP
                    m = KM + NPROJ + 1 + g
                    free_bank(n, m)
                    for k in range(G):
                        mm = nc.tensor.matmul(front[m % FB][:], w_dt[:, k, g * P:(g + 1) * P], u[:, b, k, :],
                                              start=(k == 0), stop=(k == G - 1))
                    mm.then_inc(front_full, 1)

            def tail_part(n, b, i):
                if i in OUT_STEPS:
                    half = OUT_STEPS.index(i)
                    pe.wait_ge(y_done, G * n + G)
                    wait(pe, residual, 2 * n + half)
                    for c in range(2):
                        tb = 2 * half + c
                        for k in range(G):
                            mm = nc.tensor.matmul(attn[:, c, :], zs[:, b, k, tb * P:(tb + 1) * P], w_out[:, k, :],
                                                  start=(k == 0), stop=(k == G - 1))
                    mm.then_inc(attn_full, 1)

            pe.wait_ge(weights_in, WEIGHTS)
            pe.wait_ge(ident_ready, 1)
            for i in range(STEPS):
                front_part(0, 0, i, 0)

            def tile(s, b):
                n = 2 * s + b
                for q in range(NQ):
                    for g in range(G):
                        i = q * G + g
                        if not is_last(s, b):
                            front_part(n + 1, 1 - b, i, s + b)
                        if i in HALVED:
                            pe.wait_ge(halved, halved_count(n, i))
                            states = [pairs[:, HALVED.index(i) % 2, k, :] for k in range(Q // 2)]
                        else:
                            pe.wait_ge(scanned, Q * (STEPS * n + i + 1))
                            states = [h[:, i % 2, k, :] for k in range(Q)]
                        if q == 0:
                            wait(pe, y_evac, G * (n - 1) + g + 1)
                        for k, hk in enumerate(states):
                            mm = nc.tensor.matmul(ysum[g][:], ident[:], hk, start=(q == 0 and k == 0),
                                                  stop=(q == NQ - 1 and k == len(states) - 1))
                        mm.then_inc(h_summed, 1)
                        if not is_first(s, b):
                            tail_part(n - 1, 1 - b, i)

            for_tiles(pe, tile)
            for i in OUT_STEPS:
                tail_part(2 * S - 1, 1, i)

        @block.vector
        def _(dve):
            dve.wait_ge(weights_in, WEIGHTS)
            dve.wait_ge(a_exp, 1)
            nc.vector.memset(state[:], 0.0).then_inc(saved, 1)
            nc.vector.memset(carry[:], 0.0).then_inc(carried, 1)
            nc.vector.tensor_scalar(a_neg[:], a_neg[:], -1.0, None, ALU.mult).then_inc(a_ready, 1)
            def front_part(n, b, i, chain):
                if i == 0:
                    dve.wait_ge(carried, 2 * n + 1)
                    wait(dve, conv_done, G * n)
                    nc.vector.tensor_copy(xh_pad[:, :, 0:NTAP - 1], carry[:, b]).then_inc(carried, 1)
                if CONV_STEP <= i < CONV_STEP + G:
                    g = i - CONV_STEP
                    dve.wait_ge(first_tap, G * n + g + 1)
                    for t in range(1, NTAP):
                        if t > 1:
                            chain[0] += 1
                            dve.wait_ge(dve_chain, chain[0])
                        last = nc.vector.scalar_tensor_tensor(
                            u[:, b, g, :], xh_pad[:, g, t:t + T], conv_w[:, g, t:t + 1], u[:, b, g, :],
                            ALU.mult, ALU.add)
                        last.then_inc(conv_done if t == NTAP - 1 else dve_chain, 1)
                    if g == G - 1:
                        nc.vector.tensor_copy(carry[:, b], xh_pad[:, :, T:T + NTAP - 1]).then_inc(carried, 1)
                if DT_STEP + 1 <= i < DT_STEP + 1 + G:
                    g = i - DT_STEP - 1
                    dve.wait_ge(act_chain, SOFT * (G * n + g) + SOFT)
                    nc.vector.scalar_tensor_tensor(dt_exp[:], dt_tmp[:], -1.0, dt_exp[:],
                                                   ALU.add, ALU.subtract).then_inc(dve_chain, 1)
                    nc.vector.scalar_tensor_tensor(dt_ln[:], dt_raw[:], 0.0, dt_ln[:],
                                                   ALU.max, ALU.add).then_inc(dve_chain, 1)
                    chain[0] += 2
                    dve.wait_ge(dve_chain, chain[0])
                    nc.vector.tensor_tensor(delta[:, b, g, :], dt_ln[:], dt_exp[:], ALU.subtract
                                            ).then_inc(delta_done, 1)
                    dve.wait_ge(delta_done, G * n + g + 1)
                    nc.vector.tensor_tensor(du[:, b, g, :], delta[:, b, g, :], u[:, b, g, :], ALU.mult
                                            ).then_inc(du_done, 1)

            def take_ysum(n, b, g):
                dve.wait_ge(h_summed, STEPS * n + STEPS)
                nc.vector.scalar_tensor_tensor(u[:, b, g, :], u[:, b, g, :], d_skip[:, g:g + 1], ysum[g][:],
                                               ALU.mult, ALU.add).then_inc(y_evac, 1)

            def tail_part(n, b, i, chain):
                for g in range(Y_GROUPS * i, min(Y_GROUPS * (i + 1), G)):
                    if g > 0:
                        take_ysum(n, b, g)
                    dve.wait_ge(y_evac, G * n + g + 1)
                    dve.wait_ge(z_gated, n + 1)
                    nc.vector.tensor_tensor(zs[:, b, g, :], u[:, b, g, :], zs[:, b, g, :], ALU.mult).then_inc(y_done, 1)
                if i in RES_STEPS:
                    half = RES_STEPS.index(i)
                    dve.wait_ge(attn_full, 2 * n + half + 1)
                    dve.wait_ge(x_used, n + 1)
                    part = r[:, 2 * half:2 * half + 2, :]
                    nc.vector.tensor_tensor(part, attn[:], part, ALU.add).then_inc(residual, 1)
                if i == NORM_STEP:
                    dve.wait_ge(residual, 2 * n + 2)
                    for c in range(TB):
                        nc.vector.bn_stats(stats[:, c], r[:, c]).then_inc(dve_chain, 1)
                    chain[0] += TB
                    dve.wait_ge(dve_chain, chain[0])
                    dve.sem_inc(dve_passed, 1)
                    for c in range(TB):
                        nc.vector.bn_aggr(mv[:, c], stats[:, c]).then_inc(dve_chain, 1)
                    chain[0] += TB
                    dve.wait_ge(dve_chain, chain[0])
                    nc.vector.tensor_scalar(rs[:, 0], mv[:, :, 1], LN_EPS, None, ALU.add).then_inc(var_ready, 1)
                if i == SCALE_STEP:
                    dve.wait_ge(rs_ln, 2 * n + 2)
                    nc.vector.tensor_tensor(rs[:, 1], rs[:, 2], rs[:, 2], ALU.mult).then_inc(dve_chain, 1)
                    chain[0] += 1
                    dve.wait_ge(dve_chain, chain[0])
                    nc.vector.tensor_tensor(rs[:, 1], rs[:, 1], rs[:, 0], ALU.mult).then_inc(dve_chain, 1)
                    chain[0] += 1
                    dve.wait_ge(dve_chain, chain[0])
                    nc.vector.tensor_scalar(rs[:, 1], rs[:, 1], -0.5, 1.5, ALU.mult, ALU.add).then_inc(dve_chain, 1)
                    chain[0] += 1
                    dve.wait_ge(dve_chain, chain[0])
                    nc.vector.tensor_tensor(rs[:, 3], rs[:, 1], rs[:, 2], ALU.mult).then_inc(dve_chain, 1)
                    chain[0] += 1
                    dve.wait_ge(dve_chain, chain[0])
                    for c in range(TB):
                        nc.vector.tensor_scalar(r[:, c], r[:, c], mv[:, c, 0:1], rs[:, 3, c:c + 1],
                                                ALU.subtract, ALU.mult).then_inc(x1_ready, 1)

            FRONT_LINKS = G * (NTAP - 2) + 2 * G
            TAIL_LINKS = 2 * TB + 4

            chain = [0]
            for i in range(STEPS):
                front_part(0, 0, i, chain)
            assert chain[0] == FRONT_LINKS

            def tile(s, b):
                n = 2 * s + b
                start = FRONT_LINKS * (n + 1) + TAIL_LINKS * (0 if is_first(s, b) else (n - 1))
                chain = [start]
                for q in range(NQ):
                    for g in range(G):
                        i = q * G + g
                        before, m = ((i - 2), n) if i >= 2 else (i - 2 + STEPS, n - 1)
                        if before in HALVED:
                            wait(dve, halved, halved_count(m, before))
                        else:
                            wait(dve, h_summed, STEPS * m + before + 1)
                        if q == 0 and g == 0:
                            dve.wait_ge(saved, 1 + STEPS * (n - 1) if not is_first(s, b) else 1)
                        for k in range(Q):
                            st = q * Q + k
                            if k % 2 == 0:
                                dve.wait_ge(drive_done, 2 * (STEPS * n + i) + k // 2 + 1)
                            if i == 0 and k == 2 and not is_first(s, b):
                                take_ysum(n - 1, 1 - b, 0)
                            dve.wait_ge(decay_done, Q * (STEPS * n + i) + k + 1)
                            nc.vector.tensor_tensor_scan(h[:, i % 2, k, :], decay[:, i % 2, k, :],
                                                         drive[:, i % 2, k, :], state[:, b, g, st:st + 1],
                                                         ALU.mult, ALU.add).then_inc(scanned, 1)
                        dve.wait_ge(scanned, Q * (STEPS * n + i + 1))
                        nc.vector.tensor_copy(state[:, b, g, q * Q:(q + 1) * Q], h[:, i % 2, :, T - 1]
                                              ).then_inc(saved, 1)
                        if i in HALVED:
                            j = HALVED.index(i) - 2
                            wait(dve, h_summed, STEPS * (n if j >= 0 else n - 1) + HALVED[j] + 1)
                            nc.vector.tensor_tensor(pairs[:, j % 2], h[:, i % 2, 0:Q // 2, :],
                                                    h[:, i % 2, Q // 2:Q, :], ALU.add).then_inc(halved, 1)
                        if not is_first(s, b):
                            tail_part(n - 1, 1 - b, i, chain)
                        if not is_last(s, b):
                            front_part(n + 1, 1 - b, i, chain)
                        if i == X_STEP:
                            wait(dve, x1_stored, 16 * n)
                            nc.vector.tensor_tensor(r[:], x_tok[:, b],
                                                    b_out[:].rearrange("p (o d) -> p o d", o=1)
                                                    .broadcast_to([P, TB, DM]), ALU.add).then_inc(x_used, 1)

            for_tiles(dve, tile)
            chain = [FRONT_LINKS * 2 * S + TAIL_LINKS * (2 * S - 1)]
            take_ysum(2 * S - 1, 1, 0)
            for i in range(STEPS):
                tail_part(2 * S - 1, 1, i, chain)


def ffn_block(nc, w, x1, out):
    NBATCH, SEQ, DM = x1.shape
    H = w["h1_w"].shape[0]
    KM = DM // P
    KH = H // P
    S = SEQ // T
    NT = NBATCH * S
    SET = 4
    STAGES = 6
    RAW = 4
    HALF = KH // 2
    OUT = HALF + 4
    NSETS = OUT + 1
    assert NSETS % 2 == 1 and HALF == SET and TB == 4 and KM == 2
    shapes = (("w1_w", KM, H), ("w2_w", KM, H), ("h1_w", KH, H), ("h2_w", KH, H), ("w3_w", KH, DM))
    pieces = [(name, o, kb) for name, kb, n_out in shapes for o in range(n_out // P)]
    TURNS = sum((kb + SET - 1) // SET for _, _, kb in pieces)

    ctx = ExitStack()
    with ctx:
        def sb(name, shape, dt=F32, stack=ctx):
            return stack.enter_context(nc.sbuf_tensor(name, shape, dt))

        def sem(name):
            return ctx.enter_context(nc.semaphore(name))

        s1 = sb("s1", [P, KH])
        s2 = sb("s2", [P, KH])
        s_h1 = sb("s_h1", [P, KH])
        s_h2 = sb("s_h2", [P, KH])
        s3 = sb("s3", [P, DM])
        ident = sb("ident2", [P, P])
        ones = sb("ones", [P, 1])
        differ = sb("differ", [P, TURNS])
        differ_all = sb("differ_all", [P, 1])
        flag = sb("flag", [1, 1], mybir.dt.int32)
        x_tok = sb("x1_tok", [P, 2, TB, DM])
        gate = sb("gate", [P, 2, T])
        r = sb("r2", [P, TB, DM])
        stats = sb("stats2", [P, TB, 6])
        mv = sb("mv2", [P, TB, 2])
        rs = sb("rs2", [P, 4, TB])

        def mode_tensors(tag, dt, parts):
            stack = ExitStack()
            with stack:
                m = {name: sb(f"{name}_{tag}", [P, kb, n_out], dt, stack) for name, kb, n_out in shapes}
                with ExitStack() as staging:
                    m["stage"] = sb(f"stage_{tag}", [P, STAGES, H], F32, staging)
                    m["junk"] = sb(f"junk_{tag}", [P, 2, T], F32, staging)
                m["xT"] = sb(f"xT_{tag}", [P, parts, KM, T], dt, stack)
                m["a"] = sb(f"act_a_{tag}", [P, parts, KH, T], dt, stack)
                m["b"] = sb(f"act_b_{tag}", [P, parts, KH, T], dt, stack)
                m["raw"] = sb(f"raw_{tag}", [P, RAW, T], F32, stack)
            return m

        split = mode_tensors("split", F32R, 2)
        whole = mode_tensors("whole", F32, 1)
        bank = [ctx.enter_context(nc.psum_tensor(f"bank{i}", [P, T], F32)) for i in range(2 * SET)]

        scales_in = sem("scales_in")
        ident_zero = sem("ident_zero2")
        ident_ready = sem("ident_ready2")
        ones_ready = sem("ones_ready")
        compared = sem("compared")
        counted = sem("counted")
        count_full = sem("count_full")
        flag_ready = sem("flag_ready")

        class Sems:
            def __init__(self, tag):
                def mode_sem(name):
                    return sem(f"{name}_{tag}")
                self.stage_in = [mode_sem(f"stage_in{i}") for i in range(STAGES)]
                self.turned = mode_sem("turned")
                self.kept = mode_sem("kept")
                self.x_loaded = [mode_sem(f"x1_loaded{i}") for i in range(2)]
                self.set_full = mode_sem("set_full")
                self.x_full = mode_sem("x_full")
                self.act_evac = mode_sem("act_evac")
                self.dve_evac = mode_sem("dve_evac")
                self.xT_high = mode_sem("xT_high")
                self.xT_ready = mode_sem("xT_ready")
                self.gate_ready = mode_sem("gate_ready")
                self.gated = mode_sem("gated")
                self.high = mode_sem("high")
                self.raw = mode_sem("raw")
                self.low = mode_sem("low")
                self.o_scaled = mode_sem("o_scaled")
                self.o_added = mode_sem("o_added")
                self.chain = mode_sem("ffn_chain")
                self.var_ready = mode_sem("var_ready2")
                self.root = mode_sem("root")
                self.y_ready = mode_sem("y_ready2")
                self.y_stored = mode_sem("y_stored")
                self.sp_passed = mode_sem("sp_passed2")
                self.dve_passed = mode_sem("dve_passed2")

        sems_split, sems_whole = Sems("split"), Sems("whole")
        block = ctx.enter_context(nc.Block())

        def wait(eng, semaphore, value):
            if not (isinstance(value, int) and value <= 0):
                eng.wait_ge(semaphore, value)

        def for_tiles(eng, body):
            for b in range(2):
                body(0, b)
            with eng.Fori(1, S - 1) as s:
                for b in range(2):
                    body(s, b)
            for b in range(2):
                body(S - 1, b)

        def is_first(s, b):
            return isinstance(s, int) and s == 0 and b == 0

        def is_last(s, b):
            return isinstance(s, int) and s == S - 1 and b == 1

        def banks(i, b):
            h = (i + b) % 2
            return bank[SET * h:SET * h + SET]

        def by_mode(eng, program):
            eng.wait_ge(flag_ready, 1)
            count = eng.value_load(flag[0:1, 0:1], min_val=0, max_val=1)
            with eng.If(count == 0):
                program(split, sems_split, 2)
            with eng.Else():
                load_weights[eng](whole, sems_whole)
                program(whole, sems_whole, 1)

        def sp_weights(m, q):
            done, after = 0, []
            for i, (name, o, kb) in enumerate(pieces):
                if i >= STAGES:
                    nc.sync.wait_ge(q.turned, after[i - STAGES])
                nc.sync.dma_start(m["stage"][:, i % STAGES, 0:kb * P], w[name][o * P:(o + 1) * P, :]
                                  ).then_inc(q.stage_in[i % STAGES], 16)
                done += (kb + SET - 1) // SET
                after.append(done)

        def pe_weights(m, q):
            t = 0
            for i, (name, o, kb) in enumerate(pieces):
                nc.tensor.wait_ge(q.stage_in[i % STAGES], 16 * (i // STAGES + 1))
                for k0 in range(0, kb, SET):
                    wait(nc.tensor, q.kept, t + 1 - 2 * SET)
                    if q is sems_split:
                        wait(nc.tensor, compared, t + 1 - 2 * SET)
                    for k in range(k0, min(k0 + SET, kb)):
                        mm = nc.tensor.transpose(bank[t % (2 * SET)][:, (k - k0) * P:(k - k0 + 1) * P],
                                                 m["stage"][:, i % STAGES, k * P:(k + 1) * P], ident[:])
                    mm.then_inc(q.turned, 1)
                    t += 1
            nc.tensor.wait_ge(q.kept, TURNS)

        def kept_weights(m):
            t = 0
            for name, o, kb in pieces:
                for k0 in range(0, kb, SET):
                    width = min(SET, kb - k0)
                    yield (t, m[name][:, k0:k0 + width, o * P:(o + 1) * P],
                           bank[t % (2 * SET)][:, 0:width * P].rearrange("p (k o) -> p k o", k=width))
                    t += 1

        def act_weights(m, q):
            for t, kept, turned in kept_weights(m):
                nc.scalar.wait_ge(q.turned, t + 1)
                nc.scalar.copy(kept, turned).then_inc(q.kept, 1)

        def nothing(m, q):
            pass

        load_weights = {nc.sync: sp_weights, nc.tensor: pe_weights, nc.scalar: act_weights, nc.vector: nothing}

        @block.sync
        def _(sp):
            for dst, src in ((s1, "w1_s"), (s2, "w2_s"), (s_h1, "h1_s"), (s_h2, "h2_s")):
                sp.dma_start(dst[:], w[src].rearrange("(k p) -> p k", p=P),
                             allow_slow_non_contiguous=True).then_inc(scales_in, 16)
            sp.dma_start(s3[:], w["w3_s"].rearrange("(o n) -> o n", o=1).broadcast_to([P, DM])
                         ).then_inc(scales_in, 16)
            sp_weights(split, sems_split)

            def program(m, q, parts):
                def load_x(s, b):
                    sp.dma_start(x_tok[:, b], x1[b, bass.ds(s * T, T), :].rearrange("(c p) d -> p c d", p=P)
                                 ).then_inc(q.x_loaded[b], 16)

                def tile(s, b):
                    n = 2 * s + b
                    sp.wait_ge(q.y_ready, TB * n + TB)
                    sp.sem_inc(q.sp_passed, 1)
                    sp.dma_start(out[b, bass.ds(s * T, T), :].rearrange("(c p) d -> p c d", p=P), r[:]
                                 ).then_inc(q.y_stored, 16)
                    if not (isinstance(s, int) and s == S - 1):
                        load_x(s + 1, b)

                load_x(0, 0)
                load_x(0, 1)
                for_tiles(sp, tile)
                sp.wait_ge(q.y_stored, 16 * NT)

            by_mode(sp, program)

        @block.gpsimd
        def _(pool):
            nc.gpsimd.memset(ident[:], 0.0).then_inc(ident_zero, 1)
            pool.wait_ge(ident_zero, 1)
            nc.gpsimd.affine_select(out=ident[:], in_=ident[:], compare_op=ALU.not_equal, fill=1.0,
                                    base=0, pattern=[[-1, P]], channel_multiplier=1).then_inc(ident_ready, 1)

        @block.tensor
        def _(pe):
            pe.wait_ge(ident_ready, 1)
            pe_weights(split, sems_split)
            pe.wait_ge(ones_ready, 1)
            pe.wait_ge(counted, 1)
            nc.tensor.matmul(bank[0][0:1, 0:1], differ_all[:], ones[:], start=True, stop=True
                             ).then_inc(count_full, 1)

            def program(m, q, parts):
                GATE_SETS = range(HALF)

                def free_set(n, i):
                    before, tile = (i - 2, n) if i >= 2 else (i - 2 + NSETS, n - 1)
                    if before in GATE_SETS:
                        wait(pe, q.dve_evac, (HALF + 1) * tile + before + 1)
                    elif before == OUT:
                        wait(pe, q.dve_evac, (HALF + 1) * tile + HALF + 1)
                    else:
                        wait(pe, q.act_evac, 4 * tile + before - HALF + 1)

                def product(dst, lhs, rhs, k, last_k):
                    for v in range(parts):
                        mm = nc.tensor.matmul(dst, lhs(v), rhs(v), start=(k == 0 and v == 0),
                                              stop=(k == last_k and v == parts - 1))
                    return mm

                def turn_x(b, s, target):
                    pe.wait_ge(q.x_loaded[b], 16 * s + 16)
                    for k in range(KM):
                        for c in range(TB):
                            mm = nc.tensor.transpose(target[k][:, c * P:(c + 1) * P],
                                                     x_tok[:, b, c, k * P:(k + 1) * P], ident[:])
                    mm.then_inc(q.x_full, 1)

                if parts == 1:
                    pe.wait_ge(q.kept, TURNS)
                turn_x(0, 0, banks(OUT, 1)[2:4])

                def tile(s, b):
                    n = 2 * s + b
                    pe.wait_ge(q.xT_ready, KM * n + KM)
                    for i in range(HALF):
                        free_set(n, i)
                        for j in range(SET):
                            name, o = ("w1_w", "w2_w")[j % 2], 2 * i + j // 2
                            for k in range(KM):
                                mm = product(banks(i, b)[j][:],
                                             lambda v: m[name][:, k, o * P:(o + 1) * P],
                                             lambda v: m["xT"][:, v, k, :], k, KM - 1)
                        mm.then_inc(q.set_full, 1)
                    for layer, (name, src) in enumerate((("h1_w", "a"), ("h2_w", "b"))):
                        for half in range(2):
                            i = HALF + 2 * layer + half
                            free_set(n, i)
                            for k in range(KH):
                                if half == 0:
                                    block_ready(n, layer, k)
                                for j in range(SET):
                                    o = half * SET + j
                                    mm = product(banks(i, b)[j][:],
                                                 lambda v: m[name][:, k, o * P:(o + 1) * P],
                                                 lambda v: m[src][:, v, k, :], k, KH - 1)
                            mm.then_inc(q.set_full, 1)
                    free_set(n, OUT)
                    if not is_last(s, b):
                        turn_x(1 - b, s + b, banks(OUT, b)[2:4])
                    for k in range(KH):
                        block_ready(n, 2, k)
                        for c in range(TB):
                            for v in range(parts):
                                mm = nc.tensor.matmul(
                                    banks(OUT, b)[c // 2][:, (c % 2) * DM:(c % 2 + 1) * DM],
                                    m["a"][:, v, k, c * P:(c + 1) * P], m["w3_w"][:, k, :],
                                    start=(k == 0 and v == 0 and c % 2 == 0),
                                    stop=(k == KH - 1 and v == parts - 1), skip_group_check=True)
                    mm.then_inc(q.set_full, 1)

                def block_ready(n, layer, k):
                    if parts == 2:
                        pe.wait_ge(q.high, 3 * KH * n + KH * layer + k + 1)
                        pe.wait_ge(q.low, 3 * KH * n + KH * layer + k + 1)
                    elif layer == 0:
                        pe.wait_ge(q.gated, KH * n + k + 1)
                    else:
                        pe.wait_ge(q.raw, 2 * KH * n + KH * (layer - 1) + k + 1)

                for_tiles(pe, tile)

            by_mode(pe, program)

        @block.scalar
        def _(act):
            act_weights(split, sems_split)
            act.wait_ge(scales_in, 16 * 5)

            def program(m, q, parts):
                def root(n):
                    act.wait_ge(q.var_ready, n + 1)
                    nc.scalar.activation(rs[:, 1], rs[:, 0], ACT.Sqrt).then_inc(q.root, 1)

                def tile(s, b):
                    n = 2 * s + b

                    def gate_high(o):
                        act.wait_ge(q.gated, KH * n + o + 1)
                        nc.scalar.copy(m["a"][:, 0, o, :], m["raw"][:, o % RAW, :]).then_inc(q.high, 1)

                    for i in range(HALF):
                        act.wait_ge(q.set_full, NSETS * n + i + 1)
                        for j in range(2):
                            o = 2 * i + j
                            wait(act, q.gated, KH * n + o - 1)
                            nc.scalar.activation(gate[:, j], banks(i, b)[2 * j][:], ACT.Silu,
                                                 scale=s1[:, o:o + 1]).then_inc(q.gate_ready, 1)
                        if parts == 2 and i > 0:
                            for j in range(2):
                                gate_high(2 * i - 2 + j)
                    if parts == 2:
                        for o in range(KH - 2, KH):
                            gate_high(o)
                    if not is_first(s, b):
                        root(n - 1)
                    for layer, (dst, scale) in enumerate((("b", s_h1), ("a", s_h2))):
                        for half in range(2):
                            i = HALF + 2 * layer + half
                            act.wait_ge(q.set_full, NSETS * n + i + 1)
                            for j in range(SET):
                                o = half * SET + j
                                src = banks(i, b)[j][:]
                                if parts == 1:
                                    nc.scalar.activation(m[dst][:, 0, o, :], src, ACT.Gelu,
                                                         scale=scale[:, o:o + 1]).then_inc(q.raw, 1)
                                    continue
                                wait(act, q.low, 3 * KH * n + KH * (layer + 1) + o - RAW + 1)
                                nc.scalar.activation(m["raw"][:, o % RAW, :], src, ACT.Gelu,
                                                     scale=scale[:, o:o + 1]).then_inc(q.raw, 1)
                                nc.scalar.activation(m[dst][:, 0, o, :], src, ACT.Gelu,
                                                     scale=scale[:, o:o + 1]).then_inc(q.high, 1)
                            if parts == 2:
                                act.wait_ge(q.high, 3 * KH * n + KH * (layer + 1) + half * SET + SET)
                            act.wait_ge(q.raw, 2 * KH * n + KH * layer + half * SET + SET)
                            act.sem_inc(q.act_evac, 1)

                for_tiles(act, tile)
                root(NT - 1)

            by_mode(act, program)

        @block.vector
        def _(dve):
            nc.vector.memset(ones[:], 1.0).then_inc(ones_ready, 1)
            for t, kept, turned in kept_weights(split):
                dve.wait_ge(sems_split.kept, t + 1)
                wait(dve, compared, t - 1)
                kb = kept.shape[1]
                nc.vector.scalar_tensor_tensor(
                    split["junk"][:, t % 2, 0:kb * P].rearrange("p (k o) -> p k o", k=kb), turned, 0.0,
                    kept.bitcast(F32), ALU.add, ALU.not_equal, accum_out=differ[:, t:t + 1]
                ).then_inc(compared, 1)
            dve.wait_ge(compared, TURNS)
            nc.vector.reduce_sum(differ_all[:], differ[:], mybir.AxisListType.X).then_inc(counted, 1)
            dve.wait_ge(count_full, 1)
            nc.vector.tensor_scalar(flag[:], bank[0][0:1, 0:1], 0.0, None, ALU.not_equal).then_inc(flag_ready, 1)
            dve.wait_ge(scales_in, 16 * 5)

            def program(m, q, parts):
                LINKS = 2 * TB + 1

                def x_parts(n, target):
                    dve.wait_ge(q.x_full, n + 1)
                    wait(dve, q.set_full, NSETS * (n - 1) + HALF)
                    for k in range(KM):
                        nc.vector.tensor_copy(m["xT"][:, 0, k, :], target[k][:]
                                              ).then_inc(q.xT_high if parts == 2 else q.xT_ready, 1)
                    if parts == 2:
                        for k in range(KM):
                            dve.wait_ge(q.xT_high, KM * n + k + 1)
                            nc.vector.tensor_tensor(m["xT"][:, 1, k, :], target[k][:],
                                                    m["xT"][:, 0, k, :].bitcast(F32), ALU.subtract
                                                    ).then_inc(q.xT_ready, 1)

                x_parts(0, banks(OUT, 1)[2:4])

                def low(n, layer, o, dst):
                    nc.vector.tensor_tensor(dst[:, 1, o, :], m["raw"][:, o % RAW, :],
                                            dst[:, 0, o, :].bitcast(F32), ALU.subtract).then_inc(q.low, 1)

                def scale_rows(n):
                    dve.wait_ge(q.root, n + 1)
                    nc.vector.reciprocal(rs[:, 2], rs[:, 1]).then_inc(q.chain, 1)
                    dve.wait_ge(q.chain, LINKS * n + LINKS)
                    for c in range(TB):
                        nc.vector.tensor_scalar(r[:, c], r[:, c], mv[:, c, 0:1], rs[:, 2, c:c + 1],
                                                ALU.subtract, ALU.mult).then_inc(q.y_ready, 1)

                def tile(s, b):
                    n = 2 * s + b

                    def gate_low(o):
                        dve.wait_ge(q.high, 3 * KH * n + o + 1)
                        low(n, 0, o, m["a"])

                    for i in range(HALF):
                        dve.wait_ge(q.set_full, NSETS * n + i + 1)
                        for j in range(2):
                            o = 2 * i + j
                            dve.wait_ge(q.gate_ready, KH * n + o + 1)
                            if parts == 2:
                                wait(dve, q.low, 3 * KH * n + o - RAW + 1)
                            dst = m["raw"][:, o % RAW, :] if parts == 2 else m["a"][:, 0, o, :]
                            nc.vector.scalar_tensor_tensor(dst, banks(i, b)[2 * j + 1][:], s2[:, o:o + 1],
                                                           gate[:, j], ALU.mult, ALU.mult).then_inc(q.gated, 1)
                        dve.wait_ge(q.gated, KH * n + 2 * i + 2)
                        dve.sem_inc(q.dve_evac, 1)
                        if parts == 2 and i > 0:
                            for j in range(2):
                                gate_low(2 * i - 2 + j)
                    if parts == 2:
                        for o in range(KH - 2, KH):
                            gate_low(o)
                    if not is_first(s, b):
                        scale_rows(n - 1)
                    if parts == 2:
                        for layer, dst in ((1, "b"), (2, "a")):
                            for o in range(KH):
                                if layer == 2 and o == SET and not is_last(s, b):
                                    x_parts(n + 1, banks(OUT, b)[2:4])
                                dve.wait_ge(q.raw, 2 * KH * n + KH * (layer - 1) + o + 1)
                                dve.wait_ge(q.high, 3 * KH * n + KH * layer + o + 1)
                                low(n, layer, o, m[dst])
                    elif not is_last(s, b):
                        x_parts(n + 1, banks(OUT, b)[2:4])
                    link = LINKS * n
                    dve.wait_ge(q.set_full, NSETS * n + OUT + 1)
                    wait(dve, q.y_stored, 16 * n)
                    for c in range(0, TB, 2):
                        nc.vector.tensor_tensor(
                            r[:, c:c + 2], banks(OUT, b)[c // 2][:].rearrange("p (c d) -> p c d", c=2),
                            s3[:].rearrange("p (o d) -> p o d", o=1).broadcast_to([P, 2, DM]), ALU.mult
                        ).then_inc(q.o_scaled, 1)
                    dve.wait_ge(q.o_scaled, TB // 2 * n + TB // 2)
                    if not is_last(s, b):
                        dve.wait_ge(q.xT_ready, KM * n + 2 * KM)
                    dve.sem_inc(q.dve_evac, 1)
                    nc.vector.tensor_tensor(r[:], r[:], x_tok[:, b], ALU.add).then_inc(q.o_added, 1)
                    dve.wait_ge(q.o_added, n + 1)
                    for c in range(TB):
                        nc.vector.bn_stats(stats[:, c], r[:, c]).then_inc(q.chain, 1)
                    dve.wait_ge(q.chain, link + TB)
                    dve.sem_inc(q.dve_passed, 1)
                    for c in range(TB):
                        nc.vector.bn_aggr(mv[:, c], stats[:, c]).then_inc(q.chain, 1)
                    dve.wait_ge(q.chain, link + 2 * TB)
                    nc.vector.tensor_scalar(rs[:, 0], mv[:, :, 1], LN_EPS, None, ALU.add).then_inc(q.var_ready, 1)

                for_tiles(dve, tile)
                scale_rows(NT - 1)

            by_mode(dve, program)


def build(nc, ins, out):
    x = ins["L0_attn_x"]
    NBATCH, SEQ, DM = x.shape
    NS = ins["L0_attn_A_log"].shape[1]
    x1 = nc.dram_tensor("x1_scratch", (NBATCH, SEQ, DM), F32).ap()
    b_scratch = nc.dram_tensor("b_scratch", (NS, T), F32).ap()
    mamba_block(nc, {k[len("L0_attn_"):]: v for k, v in ins.items() if "attn" in k}, x, x1, b_scratch)
    ffn_block(nc, {k[len("L0_ffn_"):]: v for k, v in ins.items() if "ffn" in k}, x1, out)


_OUT = ((2, 4096, 256), "float32")


def kernel(**inputs):
    import numpy as _np
    import concourse.bacc as _bacc
    from concourse import mybir as _mybir
    from concourse.bass_utils import run_bass_kernel_spmd as _run

    nc = _bacc.Bacc("TRN2", target_bir_lowering=False, num_devices=1)
    arrays, ins = {}, {}
    for name in inputs:
        a = _np.ascontiguousarray(inputs[name])
        arrays[f"in_{name}"] = a
        ins[name] = nc.dram_tensor(f"in_{name}", a.shape, _mybir.dt.from_np(a.dtype), kind="ExternalInput").ap()
    out = nc.dram_tensor("out_0", _OUT[0], _mybir.dt.from_np(_np.dtype(_OUT[1])), kind="ExternalOutput").ap()
    build(nc, ins, out)
    r = _run(nc, [arrays], core_ids=[0])
    return r.results[0]["out_0"]
```
